# Optimizing a Trainium2 kernel written in Bass

```python
import numpy as np
import jax
import jax.numpy as jnp

def _softmax(x, axis=-1):
    return jax.nn.softmax(x, axis=axis)

def _gelu(x):
    return jax.nn.gelu(x, approximate=True)

def _silu(x):
    return jax.nn.silu(x)

def _sigmoid(x):
    return jax.nn.sigmoid(x)

def _layernorm(x, axis=-1, eps=1e-05):
    m = jnp.mean(x, axis=axis, keepdims=True)
    v = jnp.var(x, axis=axis, keepdims=True)
    return (x - m) / jnp.sqrt(v + eps)

def _scatter_add(tgt, idx, src, axis=0):
    return tgt.at[idx].add(src)

def _segment_sum(src, seg, n):
    return jax.ops.segment_sum(src, seg, n)
kernel_name = 'mk_adj_ffn_d2_adj_r2_dfde24'

def setup_inputs(seed: int=0):
    np.random.seed(seed)
    _w = jnp.asarray

    def _rec_inputs():
        import jax
        import jax.numpy as jnp
        _gk = jax.random.key(seed)
        x = -0.0002928 + 1 * jax.random.normal(jax.random.fold_in(_gk, 1), (128, 64, 128), jnp.float32)
        _w = (1.0 + jnp.arange(64, dtype=jnp.float32)) ** (-0.5)
        _w = _w / _w.mean()
        _pij = jnp.clip(0.0625 * _w[:, None] * _w[None, :], 0.0, 1.0)
        _a = jax.random.uniform(jax.random.fold_in(_gk, 2), (128, 64, 64)) < _pij
        adj = _a.astype(jnp.int32)
        return (x, adj)
    x, adj = _rec_inputs()

    def _L0_gnn_setup():
        import jax, jax.numpy as jnp
        import numpy as np
        NEG_INF = -1000000000.0
        LEAKY_SLOPE = 0.2
        key = jax.random.key(seed)
        k1, k2, k3, k4, k5 = jax.random.split(key, 5)
        B, N, F_in, F_out = (8, 1024, 128, 128)
        x = jax.random.normal(k1, (B, N, F_in), dtype=jnp.float32)
        adj = jax.random.randint(k2, (B, N, N), 0, 2, dtype=jnp.int32)
        W = jax.random.normal(k3, (F_out, F_in), dtype=jnp.float32) * 0.05
        a_src = jax.random.normal(k4, (F_out,), dtype=jnp.float32) * 0.05
        a_dst = jax.random.normal(k5, (F_out,), dtype=jnp.float32) * 0.05
        return {'x': x, 'adj': adj, 'W': W, 'a_src': a_src, 'a_dst': a_dst}
    _L0_gnn_all = _L0_gnn_setup()
    _L0_gnn_in = {k: v for k, v in _L0_gnn_all.items() if k in ('W', 'a_src', 'a_dst')}
    del _L0_gnn_all

    def _L0_ffn_setup():
        import jax, jax.numpy as jnp
        import numpy as np
        TOP_K = 2
        LN_EPS = 1e-05
        key = jax.random.key(seed)
        ks = jax.random.split(key, 8)
        B, S, D, E, H = (16, 512, 128, 8, 512)
        x = jax.random.normal(ks[0], (B, S, D), dtype=jnp.float32)
        Wr = jax.random.normal(ks[1], (D, E), dtype=jnp.float32) * 0.1
        br = jnp.zeros((E,), dtype=jnp.float32)
        ln_g = jnp.ones((E, D), dtype=jnp.float32)
        ln_b = jnp.zeros((E, D), dtype=jnp.float32)
        W1 = jax.random.normal(ks[2], (E, D, H), dtype=jnp.float32) * (1.0 / np.sqrt(D))
        b1 = jnp.zeros((E, H), dtype=jnp.float32)
        W2 = jax.random.normal(ks[3], (E, H, D), dtype=jnp.float32) * (1.0 / np.sqrt(H))
        b2 = jnp.zeros((E, D), dtype=jnp.float32)
        return {'x': x, 'Wr': Wr, 'br': br, 'ln_g': ln_g, 'ln_b': ln_b, 'W1': W1, 'b1': b1, 'W2': W2, 'b2': b2}
    _L0_ffn_all = _L0_ffn_setup()
    _L0_ffn_in = {k: v for k, v in _L0_ffn_all.items() if k in ('Wr', 'br', 'ln_g', 'ln_b', 'W1', 'b1', 'W2', 'b2')}
    del _L0_ffn_all

    def _L1_gnn_setup():
        import jax, jax.numpy as jnp
        import numpy as np
        NEG_BIG = -9000000000000000.0
        key = jax.random.key(seed)
        k1, k2, k3, k4 = jax.random.split(key, 4)
        B, N, F_in, F_out = (4, 2048, 128, 128)
        h = jax.random.normal(k1, (B, N, F_in), dtype=jnp.float32)
        adj = jax.random.randint(k2, (B, N, N), 0, 2, dtype=jnp.int32)
        bW = 1.414 * np.sqrt(6.0 / (F_in + F_out))
        W = jax.random.uniform(k3, (F_in, F_out), minval=-bW, maxval=bW, dtype=jnp.float32)
        ba = 1.414 * np.sqrt(6.0 / (2 * F_out + 1))
        a = jax.random.uniform(k4, (2 * F_out, 1), minval=-ba, maxval=ba, dtype=jnp.float32)
        return {'h': h, 'adj': adj, 'W': W, 'a': a}
    _L1_gnn_all = _L1_gnn_setup()
    _L1_gnn_in = {k: v for k, v in _L1_gnn_all.items() if k in ('W', 'a')}
    del _L1_gnn_all

    def _L1_ffn_setup():
        import jax, jax.numpy as jnp
        import numpy as np
        B, T, D, H, E = (16, 2048, 128, 256, 8)
        key = jax.random.key(seed)
        ks = jax.random.split(key, 5)
        x = jax.random.normal(ks[0], (B, T, D), dtype=jnp.float32)
        gate_w = jax.random.normal(ks[1], (D, E), dtype=jnp.float32) * 0.02
        gate_b = jnp.zeros((E,), dtype=jnp.float32)
        W1 = jax.random.normal(ks[2], (E, D, H), dtype=jnp.float32) * 0.02
        b1 = jnp.zeros((E, H), dtype=jnp.float32)
        W2 = jax.random.normal(ks[3], (E, H, D), dtype=jnp.float32) * 0.02
        b2 = jnp.zeros((E, D), dtype=jnp.float32)
        return {'x': x, 'gate_w': gate_w, 'gate_b': gate_b, 'W1': W1, 'b1': b1, 'W2': W2, 'b2': b2}
    _L1_ffn_all = _L1_ffn_setup()
    _L1_ffn_in = {k: v for k, v in _L1_ffn_all.items() if k in ('gate_w', 'gate_b', 'W1', 'b1', 'W2', 'b2')}
    del _L1_ffn_all
    return {'x': x, 'adj': adj, 'L0_gnn_W': _L0_gnn_in['W'], 'L0_gnn_a_src': _L0_gnn_in['a_src'], 'L0_gnn_a_dst': _L0_gnn_in['a_dst'], 'L0_ffn_Wr': _L0_ffn_in['Wr'], 'L0_ffn_br': _L0_ffn_in['br'], 'L0_ffn_ln_g': _L0_ffn_in['ln_g'], 'L0_ffn_ln_b': _L0_ffn_in['ln_b'], 'L0_ffn_W1': _L0_ffn_in['W1'], 'L0_ffn_b1': _L0_ffn_in['b1'], 'L0_ffn_W2': _L0_ffn_in['W2'], 'L0_ffn_b2': _L0_ffn_in['b2'], 'L1_gnn_W': _L1_gnn_in['W'], 'L1_gnn_a': _L1_gnn_in['a'], 'L1_ffn_gate_w': _L1_ffn_in['gate_w'], 'L1_ffn_gate_b': _L1_ffn_in['gate_b'], 'L1_ffn_W1': _L1_ffn_in['W1'], 'L1_ffn_b1': _L1_ffn_in['b1'], 'L1_ffn_W2': _L1_ffn_in['W2'], 'L1_ffn_b2': _L1_ffn_in['b2']}

def reference(x, adj, L0_gnn_W, L0_gnn_a_src, L0_gnn_a_dst, L0_ffn_Wr, L0_ffn_br, L0_ffn_ln_g, L0_ffn_ln_b, L0_ffn_W1, L0_ffn_b1, L0_ffn_W2, L0_ffn_b2, L1_gnn_W, L1_gnn_a, L1_ffn_gate_w, L1_ffn_gate_b, L1_ffn_W1, L1_ffn_b1, L1_ffn_W2, L1_ffn_b2):
    import jax
    import jax.numpy as jnp

    def _L0_gnn_ref(x, adj, W, a_src, a_dst):
        import jax, jax.numpy as jnp
        import numpy as np
        NEG_INF = -1000000000.0
        LEAKY_SLOPE = 0.2
        h = jnp.einsum('bnf,of->bno', x, W)
        s_src = h @ a_src
        s_dst = h @ a_dst
        e = s_src[:, :, None] + s_dst[:, None, :]
        e = jax.nn.leaky_relu(e, negative_slope=LEAKY_SLOPE)
        e = jnp.where(adj == 0, jnp.float32(NEG_INF), e)
        alpha = jax.nn.softmax(e, axis=-1)
        h_prime = jnp.einsum('bij,bjo->bio', alpha, h)
        return h_prime

    def _L0_ffn_ref(x, Wr, br, ln_g, ln_b, W1, b1, W2, b2):
        import jax, jax.numpy as jnp
        import numpy as np
        TOP_K = 2
        LN_EPS = 1e-05
        B, S, D = x.shape
        N = B * S
        xt = x.reshape(N, D)
        logits = xt @ Wr + br
        probs = jax.nn.softmax(logits, axis=-1)
        top_p, top_idx = jax.lax.top_k(probs, TOP_K)
        weights = top_p / top_p.sum(axis=-1, keepdims=True)
        mu = xt.mean(axis=-1, keepdims=True)
        var = ((xt - mu) ** 2).mean(axis=-1, keepdims=True)
        xn = (xt - mu) * jax.lax.rsqrt(var + LN_EPS)
        xe = xn[None, :, :] * ln_g[:, None, :] + ln_b[:, None, :]
        h = jax.nn.gelu(jnp.einsum('end,edh->enh', xe, W1) + b1[:, None, :], approximate=False)
        y = jnp.einsum('enh,ehd->end', h, W2) + b2[:, None, :]
        y_tok = jnp.transpose(y, (1, 0, 2))
        sel = jnp.take_along_axis(y_tok, top_idx[:, :, None], axis=1)
        out = (weights[:, :, None] * sel).sum(axis=1)
        return out.reshape(B, S, D)

    def _L1_gnn_ref(h, adj, W, a):
        import jax, jax.numpy as jnp
        import numpy as np
        NEG_BIG = -9000000000000000.0
        F_out = W.shape[1]
        Wh = jnp.einsum('bnf,fo->bno', h, W)
        src = Wh @ a[:F_out, 0]
        dst = Wh @ a[F_out:, 0]
        e = jax.nn.leaky_relu(src[:, :, None] + dst[:, None, :], negative_slope=0.2)
        scores = jnp.where(adj > 0, e, jnp.float32(NEG_BIG))
        attention = jax.nn.softmax(scores, axis=2)
        h_prime = jnp.einsum('bij,bjo->bio', attention, Wh)
        return jax.nn.relu(h_prime)

    def _L1_ffn_ref(x, gate_w, gate_b, W1, b1, W2, b2):
        import jax, jax.numpy as jnp
        import numpy as np
        B, T, D, H, E = (16, 2048, 128, 256, 8)
        Bb, Tt, Dd = x.shape
        Ee = gate_w.shape[1]
        xf = x.reshape(-1, Dd)
        N = xf.shape[0]
        logits = xf @ gate_w + gate_b
        probs = jax.nn.softmax(logits, axis=-1)
        top2_vals, top2_idx = jax.lax.top_k(probs, 2)
        cw = jnp.zeros((N, Ee), dtype=xf.dtype).at[jnp.arange(N)[:, None], top2_idx].add(top2_vals)

        def step(acc, params):
            w1, bb1, w2, bb2, we = params
            h = jax.nn.gelu(xf @ w1 + bb1, approximate=False)
            y = h @ w2 + bb2
            return (acc + we[:, None] * y, None)
        out, _ = jax.lax.scan(step, jnp.zeros_like(xf), (W1, b1, W2, b2, cw.T))
        return out.reshape(Bb, Tt, Dd)
    x = x + _L0_gnn_ref(_layernorm(x, axis=-1), adj, L0_gnn_W, L0_gnn_a_src, L0_gnn_a_dst)
    x = x + _L0_ffn_ref(_layernorm(x, axis=-1), L0_ffn_Wr, L0_ffn_br, L0_ffn_ln_g, L0_ffn_ln_b, L0_ffn_W1, L0_ffn_b1, L0_ffn_W2, L0_ffn_b2)
    x = x + _L1_gnn_ref(_layernorm(x, axis=-1), adj, L1_gnn_W, L1_gnn_a)
    x = x + _L1_ffn_ref(_layernorm(x, axis=-1), L1_ffn_gate_w, L1_ffn_gate_b, L1_ffn_W1, L1_ffn_b1, L1_ffn_W2, L1_ffn_b2)
    return x

_drawn_inputs = setup_inputs


def setup_inputs(seed=0):
    import zlib

    import numpy as np

    out = dict(_drawn_inputs(seed))
    spreads = {'L0_ffn_br': (0.0, 0.1),
     'L0_ffn_ln_g': (1.0, 0.2),
     'L0_ffn_ln_b': (0.0, 0.1),
     'L0_ffn_b1': (0.0, 0.1),
     'L0_ffn_b2': (0.0, 0.1),
     'L1_ffn_gate_b': (0.0, 0.8),
     'L1_ffn_b1': (0.0, 0.8),
     'L1_ffn_b2': (0.0, 0.477)}
    factors = {'L1_ffn_gate_w': 3.644, 'L1_ffn_W1': 8.0, 'L1_ffn_W2': 8.0}
    for name, (base, spread) in spreads.items():
        noise = np.random.default_rng([zlib.crc32(name.encode()), seed]).standard_normal(out[name].shape)
        drawn = base * np.exp(spread * noise) if base else spread * noise
        out[name] = jnp.asarray(drawn.astype(out[name].dtype))
    for name, factor in factors.items():
        out[name] = (out[name] * factor).astype(out[name].dtype)
    return out
```

```python
from contextlib import ExitStack

import concourse.bass as bass
from concourse import mybir

ALU = mybir.AluOpType
ACT = mybir.ActivationFunctionType
AX_X = mybir.AxisListType.X
F32 = mybir.dt.float32
F16 = mybir.dt.float16
BF16 = mybir.dt.bfloat16
I32 = mybir.dt.int32
U32 = mybir.dt.uint32

P = 128
D = 128
NODES = 64
N_TOK = 128 * NODES
TILES = 8
BLK = TILES * P
NBLK = N_TOK // BLK
NE = 8
TOP = 2
GRP = 256
GT = GRP // P
NG = 72
CAP = N_TOK + GRP
SPARE = NG * GRP - N_TOK * TOP
ROWS = NE * CAP + SPARE
ROW_W = D + 2
NO_TOKEN = 4 * N_TOK
AHEAD = 4
TURNS = NG // AHEAD - 1
EPS = 1e-5
S_X, S_W, S_H = 1024.0, 64.0, 32.0
HID = [512, 256]
MASKED = [-1.0e9, -9.0e15]
BIG = 3.0e38
C_ID, C_TRI, C_REV, C_TOK, C_BASE, C_G, C_END = 0, 128, 256, 320, 328, 336, 336 + NG


class Chain:

    def __init__(self, eng, sem):
        self.eng, self.sem, self.base, self.k = eng, sem, 0, 0

    def did(self, ins):
        ins.then_inc(self.sem, 1)
        self.k += 1

    def wait(self):
        self.eng.wait_ge(self.sem, self.base + self.k)

    def loop(self, i, first, per):
        self.start = self.base + self.k
        self.base, self.k = self.start + (i - first) * per, 0

    def looped(self, turns, per):
        assert self.k == per, ("signals of a turn", self.k)
        self.base, self.k = self.start + turns * per, 0


def wait_past(eng, sem, value):
    if not (isinstance(value, int) and value <= 0):
        eng.wait_ge(sem, value)


class LayerSems:

    def __init__(self, sem, sems, L):
        self.x_in, self.x_done = sems(f"x_in{L}"), sems(f"x_done{L}")
        self.ve, self.rs = sems(f"ve{L}", 3), sems(f"rs{L}", 3)
        self.xn_ready, self.xT_ps, self.xT_sb = sem(f"xn_ready{L}"), sem(f"xT_ps{L}"), sem(f"xT_sb{L}")
        self.e_ps, self.e_copied, self.e_ready = sem(f"e_ps{L}"), sem(f"e_copied{L}"), sem(f"e_ready{L}")
        self.hs_ps, self.hs_sb = sem(f"hs_ps{L}"), sem(f"hs_sb{L}")
        self.E_sb, self.ET_ps, self.ET_sb = sem(f"E_sb{L}"), sem(f"ET_ps{L}"), sem(f"ET_sb{L}")
        self.att_ps, self.rinv_ready, self.hp_ready = sem(f"att_ps{L}"), sem(f"rinv_ready{L}"), sem(f"hp_ready{L}")
        self.xt_ready, self.xtT_ps, self.xtT_sb = sem(f"xt_ready{L}"), sem(f"xtT_ps{L}"), sem(f"xtT_sb{L}")
        self.lg_done, self.rx_ready, self.rexp = sem(f"lg_done{L}"), sem(f"rx_ready{L}"), sem(f"rexp{L}")
        self.hot_ready, self.rank_done = sem(f"hot_ready{L}"), sem(f"rank_done{L}")
        self.slots_ready, self.x1w_ready = sem(f"slots_ready{L}"), sem(f"x1w_ready{L}")
        self.scattered, self.stored = sems(f"scattered{L}"), sems(f"stored{L}")
        self.tables, self.pads_out = sem(f"tables{L}"), sem(f"pads_out{L}")
        self.g_loaded, self.y_out = sems(f"g_loaded{L}_", AHEAD), sems(f"y_out{L}_", AHEAD)
        self.gT_ps, self.gT_sb = sem(f"gT_ps{L}"), sem(f"gT_sb{L}")
        self.h_ps, self.act_done, self.h_split = sem(f"h_ps{L}"), sem(f"act_done{L}"), sem(f"h_split{L}")
        self.y_done, self.y_ready, self.placed = sem(f"y_done{L}"), sem(f"y_ready{L}"), sem(f"placed{L}")


DVE_SIGNALS = [86, 74]
ACT_CHAIN_BASE = [0, 3 * NBLK]


def gnn_moe_kernel(nc, x, adj, gW0, a_src, a_dst, Wr0, br0, ln_g, ln_b, W1_0, b1_0, W2_0, b2_0,
                   gW1, a_1, Wr1, br1, W1_1, b1_1, W2_1, b2_1, consts, out):
    NC = [h // P for h in HID]

    row_buf = [nc.dram_tensor(f"row_buf{L}", [ROWS, ROW_W], F32, kind="Internal").ap() for L in range(2)]
    x1_buf = [nc.dram_tensor(f"x1_buf{L}", [N_TOK, ROW_W], F32, kind="Internal").ap() for L in range(2)]
    y_buf = [nc.dram_tensor(f"y_buf{L}", [TOP * N_TOK, D], F32, kind="Internal").ap() for L in range(2)]
    Wr, br, b2 = [Wr0, Wr1], [br0, br1], [b2_0, b2_1]
    W1, W2 = [W1_0, W1_1], [W2_0, W2_1]

    with ExitStack() as ctx:
        def sb(name, shape, dt=F32):
            return ctx.enter_context(nc.sbuf_tensor(name, shape, dt))

        def sem(name):
            return ctx.enter_context(nc.semaphore(name))

        def sems(name, n=2):
            return [sem(f"{name}{k}") for k in range(n)]

        cst = sb("cst", [P, C_END])
        ident = cst[:, C_ID:C_ID + P]
        ident16 = sb("ident16", [P, P], F16)
        tri16 = sb("tri16", [P, P], BF16)
        ones16 = sb("ones16", [P, P], BF16)
        ones = sb("ones", [P, 1])
        vec_rows = sb("vec_rows", [68, P])
        vec_cols = sb("vec_cols", [P, 68])
        V_B1, V_G, V_B, V_A = [0, 32], 48, 56, 64
        att_vec = sb("att_vec", [P, 4, NODES])
        gw = [sb(f"gw{L}", [P, P]) for L in range(2)]
        gwT = [sb(f"gwT{L}", [P, P]) for L in range(2)]
        to_score = sb("to_score", [P, 4, NODES])
        wr = [sb(f"wr{L}", [P, NE]) for L in range(2)]
        br_bc = [sb(f"br_bc{L}", [P, NE]) for L in range(2)]
        b2_bc = [sb(f"b2_bc{L}", [P, NE, D]) for L in range(2)]
        gain = sb("gain", [P, NE])
        b1_cols = [sb("b1_cols0", [P, NE * NC[0]]), sb("b1_cols1", [P, NE * NC[1]])]
        w1 = [sb(f"w1_{L}", [P, NE, 2, HID[L]], F16) for L in range(2)]
        w2 = [sb(f"w2_{L}", [P, NE, NC[L], 2, D], F16) for L in range(2)]
        w_stage = sb("w_stage", [P, NE * 512])

        xin = [sb(f"xin{q}", [P, TILES, ROW_W]) for q in range(2)]
        yin = [sb(f"yin{q}", [P, TOP, TILES, D]) for q in range(2)]
        adj_in = [sb(f"adj_in{q}", [P, TILES, NODES], I32) for q in range(2)]
        stat = sb("stat", [P, TILES, 6])
        msum, mdif, m2s, mdif2, mean, var, ve, ln_v, rs0, nt1, nt2, rstd = (
            sb(n, [P, TILES]) for n in ("msum", "mdif", "m2s", "mdif2", "mean", "var", "ve", "ln_v", "rs0",
                                        "nt1", "nt2", "rstd"))
        xn = sb("xn", [P, TILES, D])
        xnT = sb("xnT", [P, TILES, P])
        keep = sb("keep", [P, TILES * NODES])
        e_sb = sb("e_sb", [P, TILES * NODES])
        e_act = sb("e_act", [P, TILES * NODES])
        e_msk = sb("e_msk", [P, TILES * NODES])
        e_max = sb("e_max", [P, TILES])
        e_dif = sb("e_dif", [P, TILES * NODES])
        pair_e = sb("pair_e", [P, TILES, P])
        pair_eT = sb("pair_eT", [P, TILES, P])
        h_sb = sb("h_sb", [P, TILES, D])
        rinv = sb("rinv", [P, TILES])
        h_new = sb("h_new", [P, TILES, D])
        x1w = [sb(f"x1w{q}", [P, TILES, ROW_W]) for q in range(2)]
        xff = sb("xff", [P, TILES, D])
        pay = [sb(f"pay{q}", [P, TILES, ROW_W]) for q in range(2)]
        slot = [sb(f"slot{q}", [P, TOP, TILES], U32) for q in range(2)]
        tok_run = sb("tok_run", [P, TILES])
        base_run = [sb(f"base_run{L}", [P, NE]) for L in range(2)]
        lg, eq1, ca, lg2, eq2, cb = (sb(n, [P, TILES, NE]) for n in ("lg", "eq1", "ca", "lg2", "eq2", "cb"))
        l_max, r1, l_max2, r2 = (sb(n, [P, TILES]) for n in ("l_max", "r1", "l_max2", "r2"))
        hot = sb("hot", [P, TOP, TILES, NE])
        hot_any = sb("hot_any", [P, TILES, NE], BF16)
        rx = sb("rx", [P, TILES, NE + 1])
        rex = sb("rex", [P, TILES, NE + 1])
        den = sb("den", [P, TILES])
        pos = sb("pos", [P, TILES, NE])
        hot_pos = sb("hot_pos", [P, TOP, TILES, NE])
        slot_f = sb("slot_f", [P, TOP, TILES])
        pad_row = sb("pad_row", [P, ROW_W])
        cnt, ng_e, one8, cum = (sb(n, [P, NE]) for n in ("cnt", "ng_e", "one8", "cum"))
        cnt_i, end_i = sb("cnt_i", [P, NE], I32), sb("end_i", [P, NE], I32)
        past = sb("past", [P, NG, NE])
        past_n = sb("past_n", [P, NG, NE])
        grp_e, grp_b, grp_c, grp_r = (sb(n, [P, NG]) for n in ("grp_e", "grp_b", "grp_c", "grp_r"))
        grp_ei, grp_ri = sb("grp_ei", [P, NG], I32), sb("grp_ri", [P, NG], I32)
        g_in = [sb(f"g_in{k}", [P, GT, ROW_W]) for k in range(AHEAD)]
        g_xT = [sb(f"g_xT{q}", [P, 2, GRP], F16) for q in range(2)]
        g_act = [sb(f"g_act{q}", [P, 4, GRP]) for q in range(2)]
        g_h = [sb(f"g_h{k}", [P, 2, 4, GRP], F16) for k in range(AHEAD)]
        g_y = [sb(f"g_y{k}", [P, GT, D]) for k in range(AHEAD)]
        g_k = sb("g_k", [P, GT])
        g_row = [sb(f"g_row{k}", [P, GT]) for k in range(AHEAD)]
        g_dst = [sb(f"g_dst{k}", [P, GT], U32) for k in range(AHEAD)]

        bank = [ctx.enter_context(nc.psum_tensor(f"bank{k}", [P, 512], F32)) for k in range(8)]
        lg_ps = bank[7][:, 0:TILES * NE]
        rank_ps = bank[7][:, 64:64 + TILES * NE]
        tot_ps = bank[7][:, 128:128 + NE]
        sum_ps = bank[7][:, 384:384 + TILES]

        cst_in, vec_in, gw_in, rt_in = sem("cst_in"), sem("vec_in"), sem("gw_in"), sem("rt_in")
        stage_in, stage_used = sem("stage_in"), sem("stage_used")
        set_ready, vecT_ps, vec_ready, set_ps, set_sb, ttl_ps = (
            sem("set_ready"), sem("vecT_ps"), sem("vec_ready"), sem("set_ps"), sem("set_sb"), sem("ttl_ps"))
        dve_chain, act_chain = sem("dve_chain"), sem("act_chain")
        bw_ps, pool_turns = sem("bw_ps"), sem("pool_turns")
        spare_out = sem("spare_out")
        w_ready = sems("w_ready")
        out_st = sems("out_st")
        fin_done, fin_in = sem("fin_done"), sems("fin_in")

        SL = []
        for L in range(2):
            s = LayerSems(sem, sems, L)
            SL.append(s)

        block = ctx.enter_context(nc.Block())

        def table_values(eng, table, g, n, top):
            at = table[0:1, g:g + n] if isinstance(g, int) else table[0:1, bass.ds(g, n)]
            return nc.values_load_multi_w_load_instructions(at, engines=[eng], min_val=0, max_val=top)[1]
        per = 2
        hid_v = [W1[L].rearrange("e d h -> d e h") for L in range(2)]
        out_v = [W2[L].rearrange("e (c p) d -> p (e c) d", p=P) for L in range(2)]

        @block.sync
        def _(sp):
            sp.dma_start(cst[:, :], consts).then_inc(cst_in, 16)
            rows = [(b1_0.rearrange("e (c p) -> (e c) p", p=P), V_B1[0]), (b1_1.rearrange("e (c p) -> (e c) p", p=P), V_B1[1]),
                    (ln_g, V_G), (ln_b, V_B), (a_src.unsqueeze(0), V_A), (a_dst.unsqueeze(0), V_A + 1),
                    (a_1.rearrange("(k p) o -> k (p o)", p=P), V_A + 2)]
            for src, at in rows:
                sp.dma_start(vec_rows[at:at + src.shape[0], :], src).then_inc(vec_in, 16)
            sp.dma_start(gw[0][:, :], gW0).then_inc(gw_in, 16)
            sp.dma_start(gw[1][:, :], gW1).then_inc(gw_in, 16)
            tok3 = lambda ap, n: ap[bass.ds(n * BLK, BLK), :].rearrange("(t p) w -> p t w", p=P)

            def load(L, n, q):
                s = SL[L]
                if L == 0:
                    sp.dma_start(xin[q][:, :, 0:D], tok3(x, n)).then_inc(s.x_in[q], 16)
                else:
                    sp.dma_start(xin[q][:, :, :], tok3(x1_buf[0], n)).then_inc(s.x_in[q], 16)
                    for k in range(TOP):
                        sp.dma_start(yin[q][:, k, :, :], y_buf[0][bass.ds(n * BLK + k * N_TOK, BLK), :].rearrange(
                            "(t p) w -> p t w", p=P)).then_inc(s.x_in[q], 16)
                sp.dma_start(adj_in[q][:, :, :], tok3(adj, n)).then_inc(s.x_in[q], 16)

            def store(L, n, q):
                sp.wait_ge(SL[L].x1w_ready, n + 1)
                sp.dma_start(tok3(x1_buf[L], n), x1w[q][:, :, :]).then_inc(SL[L].stored[q], 16)

            def blocks(L):
                s = SL[L]
                for n in range(2):
                    load(L, n, n)
                if L == 0:
                    for w, b, r, bb in ((wr, br_bc, b2_bc, 0), (wr, br_bc, b2_bc, 1)):
                        sp.dma_start(w[bb][:, :], Wr[bb]).then_inc(rt_in, 16)
                        sp.dma_start(b[bb][:, :], br[bb].unsqueeze(0).to_broadcast([P, NE])).then_inc(rt_in, 16)
                        sp.dma_start(r[bb][:, :, :], b2[bb].unsqueeze(0).to_broadcast([P, NE, D])).then_inc(rt_in, 16)
                    sp.wait_ge(set_ready, 1)
                    for LL in range(2):
                        sp.dma_start(row_buf[LL][NE * CAP:ROWS, :].rearrange("(t p) w -> p t w", p=P),
                                     pad_row[:, :].unsqueeze(1).to_broadcast([P, SPARE // P, ROW_W])).then_inc(spare_out, 16)
                stages = [(hid_v[L], NE * HID[L]), (out_v[L], NE * NC[L] * D)]

                def load_stage(m):
                    k = 2 * L + m
                    if k:
                        sp.wait_ge(stage_used, k)
                    src, width = stages[m]
                    sp.dma_start(w_stage[:, 0:width].rearrange("p (a b) -> p a b", a=src.shape[1]), src).then_inc(stage_in, 16)
                load_stage(0)
                with sp.Fori(0, NBLK // per - 1) as i:
                    for q in range(2):
                        n = per * i + q
                        store(L, n, q)
                        sp.wait_ge(s.x_done[q], i + 1)
                        load(L, n + per, q)
                for q in range(2):
                    store(L, NBLK - per + q, q)
                load_stage(1)

            def groups(L):
                s = SL[L]
                for q in range(2):
                    sp.wait_ge(s.scattered[q], 16 * TOP * TILES * NBLK // 2)
                sp.wait_ge(s.tables, 1)
                for e in range(NE):
                    end = sp.value_load(end_i[0:1, e:e + 1], min_val=0, max_val=NE * CAP - GRP)
                    sp.dma_start(row_buf[L][bass.ds(end, GRP), :].rearrange("(t p) w -> p t w", p=P),
                                 pad_row[:, :].unsqueeze(1).to_broadcast([P, GT, ROW_W])).then_inc(s.pads_out, 16)
                sp.wait_ge(s.pads_out, 16 * NE)
                if L == 0:
                    sp.wait_ge(spare_out, 32)

                def load_group(g, k):
                    r = sp.value_load(grp_ri[0:1, bass.ds(g, 1)], min_val=0, max_val=ROWS - GRP)
                    sp.dma_start(g_in[k][:, :, :], row_buf[L][bass.ds(r, GRP), :].rearrange("(t p) w -> p t w", p=P)
                                 ).then_inc(s.g_loaded[k], 16)
                for k in range(AHEAD):
                    load_group(k, k)
                with sp.Fori(0, TURNS) as i:
                    for k in range(AHEAD):
                        g = AHEAD * i + k
                        sp.wait_ge(s.gT_ps, g + 1)
                        sp.wait_ge(s.placed, g + 1)
                        load_group(g + AHEAD, k)

            def all_written(L):
                for k in range(AHEAD):
                    sp.wait_ge(SL[L].y_out[k], 16 * GT * NG // AHEAD)
                for q in range(2):
                    sp.wait_ge(SL[L].stored[q], 16 * NBLK // 2)

            blocks(0)
            groups(0)
            all_written(0)
            blocks(1)
            groups(1)
            all_written(1)

            def load_last(n, q):
                sp.dma_start(xin[q][:, :, :], tok3(x1_buf[1], n)).then_inc(fin_in[q], 16)
                for k in range(TOP):
                    sp.dma_start(yin[q][:, k, :, :], y_buf[1][bass.ds(n * BLK + k * N_TOK, BLK), :].rearrange(
                        "(t p) w -> p t w", p=P)).then_inc(fin_in[q], 16)

            def store_last(n, q):
                sp.wait_ge(fin_done, n + 1)
                sp.dma_start(tok3(out, n), xin[q][:, :, 0:D]).then_inc(out_st[q], 16)
            for n in range(2):
                load_last(n, n)
            with sp.Fori(0, NBLK // per - 1) as i:
                for q in range(2):
                    n = per * i + q
                    store_last(n, q)
                    sp.wait_ge(out_st[q], 16 * (i + 1))
                    load_last(n + per, q)
            for q in range(2):
                store_last(NBLK - per + q, q)
            for q in range(2):
                sp.wait_ge(out_st[q], 16 * NBLK // 2)

        @block.gpsimd
        def _(pool):
            for L in range(2):
                s = SL[L]
                with pool.Fori(0, NBLK // per) as i:
                    for q in range(2):
                        pool.wait_ge(s.slots_ready, per * i + q + 1)
                        pool.sem_inc(pool_turns, 1)
                        for k in range(TOP):
                            for t in range(TILES):
                                pool.indirect_dma_start(
                                    row_buf[L][:, :], bass.IndirectOffsetOnAxis(ap=slot[q][:, k, t:t + 1], axis=0),
                                    pay[q][:, t, :], None).then_inc(s.scattered[q], 16)
                with pool.Fori(0, NG // AHEAD) as i:
                    for k in range(AHEAD):
                        pool.wait_ge(s.y_ready, AHEAD * i + k + 1)
                        pool.sem_inc(pool_turns, 1)
                        for t in range(GT):
                            pool.indirect_dma_start(
                                y_buf[L][:, :], bass.IndirectOffsetOnAxis(ap=g_dst[k][:, t:t + 1], axis=0),
                                g_y[k][:, t, :], None, bounds_check=TOP * N_TOK - 1, oob_is_err=False
                            ).then_inc(s.y_out[k], 16)

        @block.tensor
        def _(pe):
            pe.wait_ge(vec_in, 16 * 7)
            pe.wait_ge(cst_in, 16)
            nc.tensor.transpose(bank[0][:, 0:68], vec_rows[:, :], ident[0:68, 0:68]).then_inc(vecT_ps, 1)
            pe.wait_ge(gw_in, 32)
            for L in range(2):
                last = nc.tensor.transpose(bank[1][:, L * P:(L + 1) * P], gw[L][:, :], ident)
            last.then_inc(set_ps, 1)
            pe.wait_ge(vec_ready, 1)
            for k in range(4):
                lhsT = gw[0] if k < 2 else gwT[1]
                last = nc.tensor.matmul(bank[2][:, k * NODES:(k + 1) * NODES], lhsT[:, :], att_vec[:, k, :],
                                        start=True, stop=True)
            last.then_inc(ttl_ps, 1)
            pe.wait_ge(set_sb, 1)
            pe.wait_ge(rt_in, 16 * 6)

            def transpose_tiles(src):
                for t in range(TILES):
                    last = nc.tensor.transpose(bank[t // 4][:, (t % 4) * P:(t % 4 + 1) * P], src[:, t, :], ident)
                return last

            def block_step(L, n):
                s = SL[L]
                w_h = gwT[0] if L == 0 else gw[1]
                pe.wait_ge(s.xn_ready, n + 1)
                transpose_tiles(xn).then_inc(s.xT_ps, 1)
                pe.wait_ge(s.xT_sb, n + 1)
                halves = xnT[:, :, :].rearrange("p t (g j) -> p t g j", g=2)
                for g in range(2):
                    nc.tensor.matmul(bank[2][g * NODES:(g + 1) * NODES, :], to_score[:, 2 * L + 1, :], halves[:, :, g, :],
                                     start=True, stop=False, skip_group_check=True)
                for t in range(TILES):
                    last = nc.tensor.matmul(bank[2][:, t * NODES:(t + 1) * NODES], xnT[:, t, :], to_score[:, 2 * L, :],
                                            start=False, stop=(t == TILES - 1), skip_group_check=True)
                last.then_inc(s.e_ps, 1)
                for t in range(TILES):
                    last = nc.tensor.matmul(bank[3 + t // 4][:, (t % 4) * P:(t % 4 + 1) * P], xnT[:, t, :], w_h[:, :],
                                            start=True, stop=True)
                last.then_inc(s.hs_ps, 1)
                pe.wait_ge(s.E_sb, n + 1)
                transpose_tiles(pair_e).then_inc(s.ET_ps, 1)
                pe.wait_ge(s.hs_sb, n + 1)
                pe.wait_ge(s.ET_sb, n + 1)
                for t in range(TILES):
                    nc.tensor.matmul(bank[5 + t // 4][:, (t % 4) * P:(t % 4 + 1) * P], pair_eT[:, t, :], h_sb[:, t, :],
                                     start=True, stop=True)
                    last = nc.tensor.matmul(sum_ps[:, t:t + 1], pair_eT[:, t, :], ones[:, :], start=True, stop=True)
                last.then_inc(s.att_ps, 1)
                pe.wait_ge(s.xt_ready, n + 1)
                transpose_tiles(xn).then_inc(s.xtT_ps, 1)
                pe.wait_ge(s.xtT_sb, n + 1)
                for t in range(TILES):
                    last = nc.tensor.matmul(lg_ps[:, t * NE:(t + 1) * NE], xnT[:, t, :], wr[L][:, :], start=True, stop=True)
                last.then_inc(s.lg_done, 1)
                pe.wait_ge(s.hot_ready, n + 1)
                hot_v = hot_any[:, :, :].rearrange("p t e -> p (t e)")
                nc.tensor.matmul(rank_ps, tri16[:, :], hot_v, start=True, stop=False, skip_group_check=True)
                for d in range(1, TILES):
                    nc.tensor.matmul(rank_ps[:, d * NE:], ones16[:, :], hot_v[:, 0:(TILES - d) * NE],
                                     start=False, stop=(d == TILES - 1), skip_group_check=True)
                for t in range(TILES):
                    last = nc.tensor.matmul(tot_ps, ones16[:, :], hot_v[:, t * NE:(t + 1) * NE],
                                            start=(t == 0), stop=(t == TILES - 1), skip_group_check=True)
                last.then_inc(s.rank_done, 1)

            def groups(L):
                s = SL[L]
                x_ps = [bank[b][:, 0:GRP].bitcast(F16).rearrange("p (h n) -> p h n", h=2) for b in (4, 7)]

                def to_feature_rows(k, turn):
                    q, turn = k % 2, turn + k // AHEAD
                    pe.wait_ge(s.g_loaded[k % AHEAD], 16 * (turn + 1))
                    rows16 = g_in[k % AHEAD][:, :, :].bitcast(F16)
                    for hl in range(2):
                        for t in range(GT):
                            last = nc.tensor.transpose(x_ps[q][:, hl, t * P:(t + 1) * P],
                                                       rows16[:, t, hl * D:(hl + 1) * D], ident16[:, :])
                    last.then_inc(s.gT_ps, 1)

                def experts(g, n):
                    return table_values(mybir.EngineType.PE, grp_ei, g, n, NE - 1)

                def up(g, q, e):
                    wait_past(pe, s.act_done, (g - 1) * NC[L])
                    pe.wait_ge(s.gT_sb, g + 1)
                    w = w1[L][:, :, :, :].rearrange("p e a h -> p (e a h)")
                    for c in range(NC[L]):
                        dst = bank[2 * q + c // 2][:, (c % 2) * GRP:(c % 2 + 1) * GRP]
                        for m, (wp, xp) in enumerate(((0, 0), (0, 1), (1, 0))):
                            last = nc.tensor.matmul(dst, w[:, bass.ds(e * (2 * HID[L]) + (wp * HID[L] + c * P), P)],
                                                    g_xT[q][:, xp, :], start=(m == 0), stop=(m == 2))
                        if c % 2:
                            last.then_inc(s.h_ps, 1)

                def down(g, k, e):
                    w = w2[L][:, :, :, :, :].rearrange("p e c a d -> p (e c a d)")
                    wait_past(pe, s.y_ready, g - 1)
                    pe.wait_ge(s.h_split, (NC[L] // 2) * (g + 1))
                    for t in range(GT):
                        m = 0
                        for c in range(NC[L]):
                            for wp, hp in ((0, 0), (0, 1), (1, 0)):
                                last = nc.tensor.matmul(
                                    bank[5 + k % 2][:, t * D:(t + 1) * D], g_h[k][:, hp, c, t * P:(t + 1) * P],
                                    w[:, bass.ds(e * (2 * HID[L]) + (2 * c + wp) * D, D)],
                                    start=(m == 0), stop=(m == 3 * NC[L] - 1))
                                m += 1
                    last.then_inc(s.y_done, 1)

                pe.wait_ge(s.tables, 1)
                pe.wait_ge(w_ready[L], 1)
                for k in range(2):
                    to_feature_rows(k, 0)
                es = experts(0, 2)
                up(0, 0, es[0])
                to_feature_rows(2, 0)
                up(1, 1, es[1])

                def turn(i, last=False):
                    es = experts(AHEAD * i, AHEAD if last else AHEAD + 2)
                    for k in range(AHEAD):
                        g = AHEAD * i + k
                        if not last or k + 3 < AHEAD:
                            to_feature_rows(k + 3, i)
                        if not last or k + 2 < AHEAD:
                            up(g + 2, k % 2, es[k + 2])
                        down(g, k, es[k])
                turn(0)
                with pe.Fori(1, TURNS) as i:
                    turn(i)
                turn(TURNS, last=True)

            for L in range(2):
                with pe.Fori(0, NBLK // per) as i:
                    for q in range(2):
                        block_step(L, per * i + q)
                if L == 0:
                    pe.wait_ge(stage_in, 16)
                    for e in range(NE):
                        for c in range(NC[0]):
                            k = e * NC[0] + c
                            last = nc.tensor.matmul(bank[0][:, k:k + 1], w_stage[:, e * HID[0] + c * P:e * HID[0] + (c + 1) * P],
                                                    vec_cols[:, V_B + e:V_B + e + 1], start=True, stop=True)
                    last.then_inc(bw_ps, 1)
                groups(L)

        @block.scalar
        def _(act):
            ch = Chain(act, act_chain)
            act.wait_ge(set_sb, 1)

            def copy_banks(b, dst):
                for k in range(2):
                    last = nc.scalar.activation(dst[:, 4 * k:4 * k + 4, :], bank[b + k][:, :].rearrange("p (t d) -> p t d", d=P),
                                                ACT.Copy)
                return last

            def rsqrt_guess(s, k, n):
                act.wait_ge(s.ve[k], n + 1)
                ch.did(nc.scalar.activation(ln_v[:, :], ve[:, :], ACT.Ln))
                ch.wait()
                nc.scalar.activation(rs0[:, :], ln_v[:, :], ACT.Exp, scale=-0.5).then_inc(s.rs[k], 1)

            def block_step(L, n):
                s = SL[L]
                rsqrt_guess(s, 0, n)
                act.wait_ge(s.xT_ps, n + 1)
                copy_banks(0, xnT).then_inc(s.xT_sb, 1)
                act.wait_ge(s.e_ps, n + 1)
                nc.scalar.activation(e_sb[:, :], bank[2][:, :], ACT.Copy).then_inc(s.e_copied, 1)
                act.wait_ge(s.hs_ps, n + 1)
                copy_banks(3, h_sb).then_inc(s.hs_sb, 1)
                act.wait_ge(s.e_ready, n + 1)
                for g in range(2):
                    r = slice(g * NODES, (g + 1) * NODES)
                    last = nc.scalar.activation(pair_e[r, :, r], e_dif[r, :].rearrange("p (t j) -> p t j", j=NODES), ACT.Exp)
                last.then_inc(s.E_sb, 1)
                act.wait_ge(s.ET_ps, n + 1)
                copy_banks(0, pair_eT).then_inc(s.ET_sb, 1)
                if L == 1:
                    act.wait_ge(s.rinv_ready, n + 1)
                    for t in range(TILES):
                        last = nc.scalar.activation(h_new[:, t, :], bank[5 + t // 4][:, (t % 4) * P:(t % 4 + 1) * P],
                                                    ACT.Relu, scale=rinv[:, t:t + 1])
                    last.then_inc(s.hp_ready, 1)
                rsqrt_guess(s, 1, n)
                act.wait_ge(s.xtT_ps, n + 1)
                copy_banks(0, xnT).then_inc(s.xtT_sb, 1)
                if L == 0:
                    rsqrt_guess(s, 2, n)
                act.wait_ge(s.rx_ready, n + 1)
                nc.scalar.activation(rex[:, :, :], rx[:, :, :], ACT.Exp).then_inc(s.rexp, 1)

            def groups(L):
                s = SL[L]
                x_ps = [bank[b][:, 0:GRP].bitcast(F16).rearrange("p (h n) -> p h n", h=2) for b in (4, 7)]

                def copy_x(g, q):
                    act.wait_ge(s.gT_ps, g + 1)
                    nc.scalar.activation(g_xT[q][:, :, :], x_ps[q], ACT.Copy).then_inc(s.gT_sb, 1)

                def gelu(g, q, e):
                    wait_past(act, s.h_split, (g - 1) * (NC[L] // 2))
                    for c in range(NC[L]):
                        if c % 2 == 0:
                            act.wait_ge(s.h_ps, NC[L] // 2 * g + c // 2 + 1)
                        nc.scalar.activation(g_act[q][:, c, :], bank[2 * q + c // 2][:, (c % 2) * GRP:(c % 2 + 1) * GRP],
                                             ACT.Gelu, bias=b1_cols[L][:, bass.ds(e * NC[L] + c, 1)],
                                             scale=1.0 / (S_X * S_W)).then_inc(s.act_done, 1)

                def experts(g, n):
                    return table_values(mybir.EngineType.Activation, grp_ei, g, n, NE - 1)
                act.wait_ge(s.tables, 1)
                act.wait_ge(w_ready[L], 1)
                for k in range(2):
                    copy_x(k, k)
                es = experts(0, 2)
                gelu(0, 0, es[0])
                copy_x(2, 0)
                gelu(1, 1, es[1])

                def turn(i, last=False):
                    n = 2 if last else AHEAD
                    es = experts(AHEAD * i + 2, n)
                    for k in range(n):
                        if not last or k == 0:
                            copy_x(AHEAD * i + k + 3, (k + 1) % 2)
                        gelu(AHEAD * i + k + 2, k % 2, es[k])
                with act.Fori(0, TURNS) as i:
                    turn(i)
                turn(TURNS, last=True)

            for L in range(2):
                with act.Fori(0, NBLK // per) as i:
                    base = ACT_CHAIN_BASE[L]
                    for q in range(2):
                        ch.base, ch.k = base + (per * i + q) * (3 - L), 0
                        block_step(L, per * i + q)
                groups(L)

        @block.vector
        def _(dve):
            ch = Chain(dve, dve_chain)
            V = nc.vector
            V.memset(ones[:, :], 1.0)
            V.memset(ones16[:, :], 1.0)
            V.memset(one8[:, :], 1.0)
            V.memset(pair_e[:, :, :], 0.0)
            ch.did(V.memset(pad_row[:, :], 0.0))
            ch.wait()
            V.memset(pad_row[:, D:D + 1], float(NO_TOKEN)).then_inc(set_ready, 1)
            dve.wait_ge(cst_in, 16)
            V.tensor_copy(ident16[:, :], ident)
            V.tensor_copy(tri16[:, :], cst[:, C_TRI:C_TRI + P])
            V.tensor_copy(tok_run[:, :], cst[:, C_TOK:C_TOK + TILES])
            for L in range(2):
                V.tensor_copy(base_run[L][:, :], cst[:, C_BASE:C_BASE + NE])
            dve.wait_ge(vecT_ps, 1)
            ch.did(V.tensor_copy(vec_cols[:, :], bank[0][:, 0:68]))
            ch.wait()
            V.tensor_scalar(gain[:, :], vec_cols[:, V_G:V_G + NE], S_W, None, ALU.mult)
            V.tensor_copy(b1_cols[1][:, :], vec_cols[:, V_B1[1]:V_B1[1] + NE * NC[1]])
            V.tensor_copy(att_vec[:, :, :], vec_cols[:, V_A:V_A + 4].unsqueeze(2).to_broadcast([P, 4, NODES]))
            dve.wait_ge(set_ps, 1)
            V.tensor_copy(gwT[0][:, :], bank[1][:, 0:P])
            V.tensor_copy(gwT[1][:, :], bank[1][:, P:2 * P]).then_inc(vec_ready, 1)
            dve.wait_ge(ttl_ps, 1)
            V.tensor_copy(to_score[:, :, :], bank[2][:, 0:4 * NODES].rearrange("p (k j) -> p k j", j=NODES)).then_inc(set_sb, 1)
            dve.wait_ge(set_sb, 1)
            dve.wait_ge(rt_in, 16 * 6)

            rev = cst[:, C_REV:C_REV + TILES * NE].rearrange("p (t e) -> p t e", e=NE)
            bc = lambda ap: ap.unsqueeze(2).to_broadcast([P, TILES, NE])

            def normalise(s, k, n, src, dst):
                for t in range(TILES):
                    last = V.bn_stats(stat[:, t, :], src[:, t, :])
                ch.did(last)
                ch.wait()
                V.tensor_tensor(msum[:, :], stat[:, :, 1], stat[:, :, 4], ALU.add)
                V.tensor_tensor(m2s[:, :], stat[:, :, 2], stat[:, :, 5], ALU.add)
                ch.did(V.tensor_tensor(mdif[:, :], stat[:, :, 1], stat[:, :, 4], ALU.subtract))
                ch.wait()
                V.tensor_scalar(mean[:, :], msum[:, :], 0.5, None, ALU.mult)
                ch.did(V.tensor_tensor(mdif2[:, :], mdif[:, :], mdif[:, :], ALU.mult))
                ch.wait()
                ch.did(V.scalar_tensor_tensor(var[:, :], mdif2[:, :], D / 4.0, m2s[:, :], ALU.mult, ALU.add))
                ch.wait()
                V.tensor_scalar(ve[:, :], var[:, :], 1.0 / D, EPS, ALU.mult, ALU.add).then_inc(s.ve[k], 1)
                dve.wait_ge(s.rs[k], n + 1)
                ch.did(V.tensor_tensor(nt1[:, :], rs0[:, :], rs0[:, :], ALU.mult))
                ch.wait()
                ch.did(V.scalar_tensor_tensor(nt2[:, :], nt1[:, :], -0.5, ve[:, :], ALU.mult, ALU.mult))
                ch.wait()
                ch.did(V.scalar_tensor_tensor(rstd[:, :], nt2[:, :], 1.5, rs0[:, :], ALU.add, ALU.mult))
                ch.wait()
                for t in range(TILES):
                    last = V.tensor_scalar(dst[:, t, :], src[:, t, :], mean[:, t:t + 1], rstd[:, t:t + 1],
                                           ALU.subtract, ALU.mult)
                return last

            def add_experts(src, y):
                for k in range(TOP):
                    for t in range(TILES):
                        last = V.scalar_tensor_tensor(src[:, t, 0:D], y[:, k, t, :], src[:, t, D + k:D + k + 1],
                                                      src[:, t, 0:D], ALU.mult, ALU.add)
                    if k == 0:
                        ch.did(last)
                        ch.wait()
                return last

            def block_step(L, i, n, q):
                s = SL[L]
                dve.wait_ge(s.x_in[q], (32 if L == 0 else 64) * (i + 1))
                src = xin[q][:, :, 0:D]
                if L == 1:
                    ch.did(add_experts(xin[q], yin[q]))
                    ch.wait()
                V.tensor_scalar(keep[:, :], adj_in[q][:, :, :].rearrange("p t j -> p (t j)"), 0.0, BIG,
                                ALU.not_equal if L == 0 else ALU.is_gt, ALU.mult)
                normalise(s, 0, n, src, xn).then_inc(s.xn_ready, 1)
                dve.wait_ge(s.e_copied, n + 1)
                ch.did(V.scalar_tensor_tensor(e_act[:, :], e_sb[:, :], 0.2, e_sb[:, :], ALU.mult, ALU.max))
                ch.wait()
                ch.did(V.scalar_tensor_tensor(e_msk[:, :], keep[:, :], MASKED[L], e_act[:, :], ALU.add, ALU.min))
                ch.wait()
                e3 = e_msk[:, :].rearrange("p (t j) -> p t j", j=NODES)
                ch.did(V.tensor_reduce(e_max[:, :], e3, AX_X, ALU.max))
                ch.wait()
                V.tensor_tensor(e_dif[:, :].rearrange("p (t j) -> p t j", j=NODES), e3,
                                e_max[:, :].unsqueeze(2).to_broadcast([P, TILES, NODES]), ALU.subtract).then_inc(s.e_ready, 1)
                dve.wait_ge(s.att_ps, n + 1)
                V.reciprocal(rinv[:, :], sum_ps).then_inc(s.rinv_ready, 1)
                wait_past(dve, s.stored[q], 16 * i)
                if L == 0:
                    dve.wait_ge(s.rinv_ready, n + 1)
                    for t in range(TILES):
                        last = V.scalar_tensor_tensor(x1w[q][:, t, 0:D], bank[5 + t // 4][:, (t % 4) * P:(t % 4 + 1) * P],
                                                      rinv[:, t:t + 1], src[:, t, :], ALU.mult, ALU.add)
                else:
                    dve.wait_ge(s.hp_ready, n + 1)
                    last = V.tensor_tensor(x1w[q][:, :, 0:D], h_new[:, :, :], src, ALU.add)
                last.then_inc(s.x_done[q], 1)
                dve.wait_ge(s.x_done[q], i + 1)
                normalise(s, 1, n, x1w[q][:, :, 0:D], xn).then_inc(s.xt_ready, 1)
                dve.wait_ge(s.xt_ready, n + 1)
                ff = xn
                if L == 0:
                    ch.did(normalise(s, 2, n, xn, xff))
                    ch.wait()
                    ff = xff
                wait_past(dve, s.scattered[q], 16 * TOP * TILES * i)
                pay16 = pay[q][:, :, :].bitcast(F16)
                V.tensor_copy(pay[q][:, :, D], tok_run[:, :])
                ch.did(V.tensor_scalar(pay16[:, :, 0:D], ff[:, :, :], S_X, None, ALU.mult))
                ch.wait()
                V.scalar_tensor_tensor(pay16[:, :, D:2 * D], ff[:, :, :], S_X, pay16[:, :, 0:D], ALU.mult, ALU.subtract)
                V.tensor_scalar(tok_run[:, :], tok_run[:, :], float(BLK), None, ALU.add)
                dve.wait_ge(s.lg_done, n + 1)
                ch.did(V.tensor_tensor(lg[:, :, :], lg_ps.rearrange("p (t e) -> p t e", e=NE),
                                       br_bc[L][:, :].unsqueeze(1).to_broadcast([P, TILES, NE]), ALU.add))

                def first_max(val, vmax, eq, cand, cmax, k):
                    ch.wait()
                    ch.did(V.tensor_reduce(vmax[:, :], val[:, :, :], AX_X, ALU.max))
                    ch.wait()
                    ch.did(V.tensor_tensor(eq[:, :, :], val[:, :, :], bc(vmax[:, :]), ALU.is_equal))
                    ch.wait()
                    ch.did(V.tensor_tensor(cand[:, :, :], eq[:, :, :], rev, ALU.mult))
                    ch.wait()
                    ch.did(V.tensor_reduce(cmax[:, :], cand[:, :, :], AX_X, ALU.max))
                    ch.wait()
                    ch.did(V.tensor_tensor(hot[:, k, :, :], cand[:, :, :], bc(cmax[:, :]), ALU.is_equal))
                first_max(lg, l_max, eq1, ca, r1, 0)
                ch.wait()
                V.tensor_scalar(pay[q][:, :, D + 1], r1[:, :], -1.0, float(NE), ALU.mult, ALU.add)
                ch.did(V.scalar_tensor_tensor(lg2[:, :, :], hot[:, 0, :, :], -BIG, lg[:, :, :], ALU.mult, ALU.add))
                first_max(lg2, l_max2, eq2, cb, r2, 1)
                ch.wait()
                V.tensor_tensor(hot_any[:, :, :], hot[:, 0, :, :], hot[:, 1, :, :], ALU.add).then_inc(s.hot_ready, 1)
                V.tensor_tensor(rx[:, :, 0:NE], lg[:, :, :], bc(l_max[:, :]), ALU.subtract)
                V.tensor_tensor(rx[:, :, NE], l_max2[:, :], l_max[:, :], ALU.subtract).then_inc(s.rx_ready, 1)
                dve.wait_ge(s.rank_done, n + 1)
                ch.did(V.tensor_tensor(pos[:, :, :], rank_ps.rearrange("p (t e) -> p t e", e=NE),
                                       base_run[L][:, :].unsqueeze(1).to_broadcast([P, TILES, NE]), ALU.add))
                ch.wait()
                V.tensor_tensor(base_run[L][:, :], base_run[L][:, :], tot_ps, ALU.add)
                for k in range(TOP):
                    last = V.tensor_tensor(hot_pos[:, k, :, :], hot[:, k, :, :], pos[:, :, :], ALU.mult)
                ch.did(last)
                ch.wait()
                ch.did(V.tensor_reduce(slot_f[:, :, :], hot_pos[:, :, :, :], AX_X, ALU.add))
                ch.wait()
                V.tensor_copy(slot[q][:, :, :], slot_f[:, :, :]).then_inc(s.slots_ready, 1)
                dve.wait_ge(s.rexp, n + 1)
                if L == 0:
                    ch.did(V.tensor_scalar(den[:, :], rex[:, :, NE], 1.0, None, ALU.add))
                else:
                    ch.did(V.tensor_reduce(den[:, :], rex[:, :, 0:NE], AX_X, ALU.add))
                ch.wait()
                ch.did(V.reciprocal(x1w[q][:, :, D], den[:, :]))
                ch.wait()
                V.tensor_tensor(x1w[q][:, :, D + 1], x1w[q][:, :, D], rex[:, :, NE], ALU.mult).then_inc(s.x1w_ready, 1)

            def group_tables(L):
                s = SL[L]
                dve.wait_ge(s.x1w_ready, NBLK)
                base0 = cst[:, C_BASE:C_BASE + NE]
                V.tensor_copy(end_i[:, :], base_run[L][:, :])
                ch.did(V.tensor_tensor(cnt[:, :], base_run[L][:, :], base0, ALU.subtract))
                ch.wait()
                ch.did(V.tensor_scalar(cnt_i[:, :], cnt[:, :], float(GRP - 1), None, ALU.add))
                ch.wait()
                ch.did(V.tensor_scalar(cnt_i[:, :], cnt_i[:, :], 8, None, ALU.logical_shift_right))
                ch.wait()
                ch.did(V.tensor_copy(ng_e[:, :], cnt_i[:, :]))
                ch.wait()
                ch.did(V.tensor_tensor_scan(cum[:, :], one8[:, :], ng_e[:, :], 0.0, ALU.mult, ALU.add))
                ch.wait()
                g_no = cst[:, C_G:C_G + NG]
                wide = [P, NG, NE]
                ch.did(V.tensor_tensor(past[:, :, :], cum[:, :].unsqueeze(1).to_broadcast(wide),
                                       g_no.unsqueeze(2).to_broadcast(wide), ALU.is_le))
                ch.wait()
                V.tensor_reduce(grp_e[:, :], past[:, :, :], AX_X, ALU.add)
                ch.did(V.tensor_tensor(past_n[:, :, :], past[:, :, :], ng_e[:, :].unsqueeze(1).to_broadcast(wide), ALU.mult))
                ch.wait()
                ch.did(V.tensor_reduce(grp_b[:, :], past_n[:, :, :], AX_X, ALU.add))
                ch.wait()
                V.tensor_scalar(grp_r[:, :], grp_e[:, :], float(CAP), None, ALU.mult)
                ch.did(V.tensor_tensor(grp_c[:, :], g_no, grp_b[:, :], ALU.subtract))
                ch.wait()
                V.tensor_scalar(grp_ei[:, :], grp_e[:, :], float(NE - 1), None, ALU.min)
                ch.did(V.scalar_tensor_tensor(grp_b[:, :], grp_c[:, :], float(GRP), grp_r[:, :], ALU.mult, ALU.add))
                ch.wait()
                V.tensor_copy(grp_ri[:, :], grp_b[:, :]).then_inc(s.tables, 1)

            def split_weights(L):
                dve.wait_ge(stage_in, 16 * (2 * L + 1))
                if L == 0:
                    dve.wait_ge(bw_ps, 1)
                    V.tensor_tensor(b1_cols[0][:, :], bank[0][:, 0:NE * NC[0]], vec_cols[:, 0:NE * NC[0]], ALU.add)
                for part in range(2):
                    for e in range(NE):
                        st = w_stage[:, e * HID[L]:(e + 1) * HID[L]]
                        scale = gain[:, e:e + 1] if L == 0 else S_W
                        if part == 0:
                            last = V.tensor_scalar(w1[L][:, e, 0, :], st, scale, None, ALU.mult)
                        else:
                            last = V.scalar_tensor_tensor(w1[L][:, e, 1, :], st, scale, w1[L][:, e, 0, :], ALU.mult, ALU.subtract)
                    if part == 0:
                        ch.did(last)
                        ch.wait()
                last.then_inc(stage_used, 1)
                dve.wait_ge(stage_in, 16 * (2 * L + 2))
                st = w_stage[:, 0:NE * NC[L] * D].rearrange("p (ec d) -> p ec d", d=D)
                hi, lo = (w2[L][:, :, :, k, :].rearrange("p e c d -> p (e c) d") for k in range(2))
                ch.did(V.tensor_scalar(hi, st, S_W, None, ALU.mult))
                ch.wait()
                V.scalar_tensor_tensor(lo, st, S_W, hi, ALU.mult, ALU.subtract).then_inc(w_ready[L], 1)
                dve.wait_ge(w_ready[L], 1)
                V.memset(g_k[:, :], 0.0).then_inc(stage_used, 1)
                dve.wait_ge(stage_used, 2 * (L + 1))

            def groups(L):
                s = SL[L]
                half = NC[L] // 2

                def place(g, k, turn):
                    dve.wait_ge(s.g_loaded[k], 16 * (turn + 1))
                    wait_past(dve, s.placed, g)
                    ch.did(V.tensor_scalar(g_k[:, :], g_in[k][:, :, D + 1], grp_e[:, bass.ds(g, 1)], float(N_TOK),
                                           ALU.not_equal, ALU.mult))
                    ch.wait()
                    V.tensor_tensor(g_row[k][:, :], g_k[:, :], g_in[k][:, :, D], ALU.add).then_inc(s.placed, 1)

                def split(g, k):
                    part = [slice(2 * hf, 2 * hf + 2) for hf in range(half)]
                    a = g_act[k % 2]
                    for hf in range(half):
                        dve.wait_ge(s.act_done, NC[L] * g + 2 * hf + 2)
                        ch.did(V.tensor_scalar(g_h[k][:, 0, part[hf], :], a[:, part[hf], :], S_H, None, ALU.mult))
                    for hf in range(half):
                        if hf == 0:
                            ch.wait()
                        V.scalar_tensor_tensor(g_h[k][:, 1, part[hf], :], a[:, part[hf], :], S_H,
                                               g_h[k][:, 0, part[hf], :], ALU.mult, ALU.subtract).then_inc(s.h_split, 1)

                def experts(g, n):
                    return table_values(mybir.EngineType.DVE, grp_ei, g, n, NE - 1)

                def finish(g, k, turn, e):
                    wait_past(dve, s.y_out[k], 16 * GT * turn)
                    dve.wait_ge(s.placed, g + 1)
                    V.tensor_copy(g_dst[k][:, :], g_row[k][:, :])
                    dve.wait_ge(s.y_done, g + 1)
                    flat = b2_bc[L][:, :, :].rearrange("p e d -> p (e d)")
                    V.scalar_tensor_tensor(g_y[k][:, :, :], bank[5 + k % 2][:, 0:GT * D].rearrange("p (t d) -> p t d", d=D),
                                           1.0 / (S_H * S_W), flat[:, bass.ds(e * D, D)].unsqueeze(1).to_broadcast([P, GT, D]),
                                           ALU.mult, ALU.add).then_inc(s.y_ready, 1)
                for k in range(2):
                    place(k, k, 0)
                    split(k, k)
                turn_signals = AHEAD * (half + 1)

                def turn(i, last=False):
                    es = experts(AHEAD * i, AHEAD)
                    for k in range(AHEAD):
                        g, a = AHEAD * i + k, (k + 2) % AHEAD
                        if not last or k + 2 < AHEAD:
                            place(g + 2, a, i + (k + 2) // AHEAD)
                            split(g + 2, a)
                        finish(g, k, i, es[k])
                turn(0)
                with dve.Fori(1, TURNS) as i:
                    ch.loop(i, 1, turn_signals)
                    turn(i)
                ch.looped(TURNS - 1, turn_signals)
                turn(TURNS, last=True)

            for L in range(2):
                for q in range(2):
                    block_step(L, 0, q, q)
                with dve.Fori(1, NBLK // per) as i:
                    ch.loop(i, 1, DVE_SIGNALS[L])
                    for q in range(2):
                        block_step(L, i, per * i + q, q)
                ch.looped(NBLK // per - 1, DVE_SIGNALS[L])
                if L == 0:
                    ch.did(V.tensor_copy(tok_run[:, :], cst[:, C_TOK:C_TOK + TILES]))
                group_tables(L)
                split_weights(L)
                groups(L)
            with dve.Fori(0, NBLK // per) as i:
                ch.loop(i, 0, 2)
                for q in range(2):
                    dve.wait_ge(fin_in[q], 48 * (i + 1))
                    add_experts(xin[q], yin[q]).then_inc(fin_done, 1)
            ch.looped(NBLK // per, 2)


_INS = ['x', 'adj', 'L0_gnn_W', 'L0_gnn_a_src', 'L0_gnn_a_dst', 'L0_ffn_Wr', 'L0_ffn_br', 'L0_ffn_ln_g', 'L0_ffn_ln_b',
        'L0_ffn_W1', 'L0_ffn_b1', 'L0_ffn_W2', 'L0_ffn_b2', 'L1_gnn_W', 'L1_gnn_a', 'L1_ffn_gate_w', 'L1_ffn_gate_b',
        'L1_ffn_W1', 'L1_ffn_b1', 'L1_ffn_W2', 'L1_ffn_b2']


def kernel(**inputs):
    import numpy as _np
    import concourse.bacc as _bacc
    from concourse import mybir as _mybir
    from concourse.bass_utils import run_bass_kernel_spmd as _run

    nc = _bacc.Bacc("TRN2", target_bir_lowering=False, num_devices=1)
    arrays, args = {}, []
    for name in _INS:
        a = _np.ascontiguousarray(inputs[name])
        if name in ('x', 'adj'):
            a = a.reshape(N_TOK, a.shape[-1])
        arrays[f"in_{name}_dram"] = a
        args.append(nc.dram_tensor(f"in_{name}_dram", a.shape, _mybir.dt.from_np(a.dtype), kind="ExternalInput").ap())
    c = _np.zeros((P, C_END), _np.float32)
    c[:, C_ID:C_ID + P] = _np.eye(P)
    c[:, C_TRI:C_TRI + P] = _np.triu(_np.ones((P, P)), 1)
    c[:, C_REV:C_REV + TILES * NE] = _np.tile(NE - _np.arange(NE), TILES)
    c[:, C_TOK:C_TOK + TILES] = _np.arange(TILES) * P + _np.arange(P)[:, None]
    c[:, C_BASE:C_BASE + NE] = _np.arange(NE) * CAP
    c[:, C_G:C_G + NG] = _np.arange(NG)
    arrays["in_consts_dram"] = c
    args.append(nc.dram_tensor("in_consts_dram", c.shape, F32, kind="ExternalInput").ap())
    args.append(nc.dram_tensor("out_0_dram", (N_TOK, D), F32, kind="ExternalOutput").ap())
    gnn_moe_kernel(nc, *args)
    r = _run(nc, [arrays], core_ids=[0])
    return r.results[0]["out_0_dram"].reshape(128, NODES, D)
```

```python
from contextlib import ExitStack

import concourse.bass as bass
from concourse import mybir

ALU = mybir.AluOpType
ACT = mybir.ActivationFunctionType
AX_X = mybir.AxisListType.X
F32 = mybir.dt.float32
F16 = mybir.dt.float16
BF16 = mybir.dt.bfloat16
I32 = mybir.dt.int32
U32 = mybir.dt.uint32

P = 128
D = 128
NODES = 64
N_TOK = 128 * NODES
TILES = 8
BLK = TILES * P
NBLK = N_TOK // BLK
NE = 8
TOP = 2
GRP = 256
GT = GRP // P
NG = 72
CAP = N_TOK + GRP
SPARE = NG * GRP - N_TOK * TOP
ROWS = NE * CAP + SPARE
ROW_W = D + 2
NO_TOKEN = 4 * N_TOK
AHEAD = 4
TURNS = NG // AHEAD - 1
EPS = 1e-5
S_X, S_W, S_H = 1024.0, 64.0, 32.0
HID = [512, 256]
MASKED = [-1.0e9, -9.0e15]
BIG = 3.0e38
C_ID, C_TRI, C_REV, C_TOK, C_BASE, C_G, C_END = 0, 128, 256, 320, 328, 336, 336 + NG


class Chain:

    def __init__(self, eng, sem):
        self.eng, self.sem, self.base, self.k = eng, sem, 0, 0

    def did(self, ins):
        ins.then_inc(self.sem, 1)
        self.k += 1

    def wait(self):
        self.eng.wait_ge(self.sem, self.base + self.k)

    def loop(self, i, first, per):
        self.start = self.base + self.k
        self.base, self.k = self.start + (i - first) * per, 0

    def looped(self, turns, per):
        assert self.k == per, ("signals of a turn", self.k)
        self.base, self.k = self.start + turns * per, 0


def wait_past(eng, sem, value):
    if not (isinstance(value, int) and value <= 0):
        eng.wait_ge(sem, value)


class LayerSems:

    def __init__(self, sem, sems, L):
        self.x_in, self.taken, self.x_done = sems(f"x_in{L}"), sem(f"taken{L}"), sem(f"x_done{L}")
        self.st1, self.st2 = sem(f"st1_{L}"), sem(f"st2_{L}")
        self.xn_ready, self.xT_ps, self.xT_sb = sem(f"xn_ready{L}"), sem(f"xT_ps{L}"), sem(f"xT_sb{L}")
        self.e_ps, self.e_copied, self.e_ready = sem(f"e_ps{L}"), sem(f"e_copied{L}"), sem(f"e_ready{L}")
        self.hs_ps, self.hs_sb = sem(f"hs_ps{L}"), sem(f"hs_sb{L}")
        self.E_sb, self.ET_ps, self.ET_sb = sem(f"E_sb{L}"), sem(f"ET_ps{L}"), sem(f"ET_sb{L}")
        self.att_ps, self.att_sb = sem(f"att_ps{L}"), sem(f"att_sb{L}")
        self.xt_ready, self.xtT_ps, self.xtT_sb = sem(f"xt_ready{L}"), sem(f"xtT_ps{L}"), sem(f"xtT_sb{L}")
        self.lg_done, self.lg_copied, self.hot_ready = sem(f"lg_done{L}"), sem(f"lg_copied{L}"), sem(f"hot_ready{L}")
        self.rexp, self.rank_done = sem(f"rexp{L}"), sem(f"rank_done{L}")
        self.ff_ready, self.hi_ready = sem(f"ff_ready{L}"), sem(f"hi_ready{L}")
        self.slots_ready, self.x1w_ready = sem(f"slots_ready{L}"), sem(f"x1w_ready{L}")
        self.scattered, self.stored = sems(f"scattered{L}"), sems(f"stored{L}")
        self.tables, self.pads_out = sem(f"tables{L}"), sem(f"pads_out{L}")
        self.g_loaded, self.y_out = sems(f"g_loaded{L}_", AHEAD), sems(f"y_out{L}_", AHEAD)
        self.gT_ps, self.gT_sb = sem(f"gT_ps{L}"), sem(f"gT_sb{L}")
        self.h_ps, self.act_done, self.h_split = sem(f"h_ps{L}"), sem(f"act_done{L}"), sem(f"h_split{L}")
        self.y_done, self.y_ready, self.placed = sem(f"y_done{L}"), sem(f"y_ready{L}"), sem(f"placed{L}")


def block_at(i, d):
    return 2 * i + d, d % 2, i + d // 2


DVE_SIGNALS = [108, 112]


def gnn_moe_kernel(nc, x, adj, gW0, a_src, a_dst, Wr0, br0, ln_g, ln_b, W1_0, b1_0, W2_0, b2_0,
                   gW1, a_1, Wr1, br1, W1_1, b1_1, W2_1, b2_1, consts, out):
    NC = [h // P for h in HID]

    row_buf = [nc.dram_tensor(f"row_buf{L}", [ROWS, ROW_W], F32, kind="Internal").ap() for L in range(2)]
    x1_buf = [nc.dram_tensor(f"x1_buf{L}", [N_TOK, ROW_W], F32, kind="Internal").ap() for L in range(2)]
    y_buf = [nc.dram_tensor(f"y_buf{L}", [TOP * N_TOK, D], F32, kind="Internal").ap() for L in range(2)]
    Wr, br, b2 = [Wr0, Wr1], [br0, br1], [b2_0, b2_1]
    W1, W2 = [W1_0, W1_1], [W2_0, W2_1]

    with ExitStack() as ctx:
        def sb(name, shape, dt=F32):
            return ctx.enter_context(nc.sbuf_tensor(name, shape, dt))

        def sem(name):
            return ctx.enter_context(nc.semaphore(name))

        def sems(name, n=2):
            return [sem(f"{name}{k}") for k in range(n)]

        cst = sb("cst", [P, C_END])
        ident = cst[:, C_ID:C_ID + P]
        ident16 = sb("ident16", [P, P], F16)
        tri16 = sb("tri16", [P, P], BF16)
        ones16 = sb("ones16", [P, P], BF16)
        vec_rows = sb("vec_rows", [68, P])
        vec_cols = sb("vec_cols", [P, 68])
        V_B1, V_G, V_B, V_A = [0, 32], 48, 56, 64
        att_vec = sb("att_vec", [P, 4, NODES])
        gw = [sb(f"gw{L}", [P, P]) for L in range(2)]
        gwT = [sb(f"gwT{L}", [P, P]) for L in range(2)]
        to_score = sb("to_score", [P, 4, NODES])
        wr = [sb(f"wr{L}", [P, NE]) for L in range(2)]
        br_bc = [sb(f"br_bc{L}", [P, NE]) for L in range(2)]
        b2_bc = [sb(f"b2_bc{L}", [P, NE, D]) for L in range(2)]
        gain = sb("gain", [P, NE])
        b1_cols = [sb("b1_cols0", [P, NE * NC[0]]), sb("b1_cols1", [P, NE * NC[1]])]
        w1 = [sb(f"w1_{L}", [P, NE, 2, HID[L]], F16) for L in range(2)]
        w2 = [sb(f"w2_{L}", [P, NE, NC[L], 2, D], F16) for L in range(2)]
        w_stage = sb("w_stage", [P, NE * 512])

        xin = [sb(f"xin{q}", [P, TILES, ROW_W]) for q in range(2)]
        yin = [sb(f"yin{q}", [P, TOP, TILES, D]) for q in range(2)]
        adj_in = [sb(f"adj_in{q}", [P, TILES, NODES], I32) for q in range(2)]
        stat = sb("stat", [P, 2 * TILES, 6])
        msum, mdif, m2s, mdif2, mean, var, ve, nt1, nt2, nt3 = (
            sb(n, [P, 2 * TILES]) for n in ("msum", "mdif", "m2s", "mdif2", "mean", "var", "ve", "nt1", "nt2", "nt3"))
        half_bits = sb("half_bits", [P, 2 * TILES], I32)
        rstd1, nmr1 = sb("rstd1", [P, 2 * TILES]), sb("nmr1", [P, 2 * TILES])
        rstd2, nmr2 = sb("rstd2", [P, TILES]), sb("nmr2", [P, TILES])
        xn = sb("xn", [P, TILES, D])
        xnT = sb("xnT", [P, TILES, P])
        xt = sb("xt", [P, TILES, D])
        xtT = sb("xtT", [P, TILES, P])
        keep = sb("keep", [P, TILES * NODES])
        e_sb = sb("e_sb", [P, TILES * NODES])
        e_act = sb("e_act", [P, TILES * NODES])
        e_msk = sb("e_msk", [P, TILES * NODES])
        e_max = sb("e_max", [P, TILES])
        e_dif = sb("e_dif", [P, TILES * NODES])
        pair_e = sb("pair_e", [P, TILES, P])
        pair_eT = sb("pair_eT", [P, TILES, P])
        h_sb = sb("h_sb", [P, TILES, D])
        sum_sb, rinv = sb("sum_sb", [P, TILES]), sb("rinv", [P, TILES])
        h_new = sb("h_new", [P, TILES, D])
        lg_raw = sb("lg_raw", [P, TILES, NE])
        x1w = [sb(f"x1w{q}", [P, TILES, ROW_W]) for q in range(2)]
        xff = sb("xff", [P, TILES, D])
        pay = [sb(f"pay{q}", [P, TILES, ROW_W]) for q in range(2)]
        slot = [sb(f"slot{q}", [P, TOP, TILES], U32) for q in range(2)]
        tok_run = sb("tok_run", [P, TILES])
        base_run = [sb(f"base_run{L}", [P, NE]) for L in range(2)]
        lg, eq1, ca, lg2, eq2, cb = (sb(n, [P, TILES, NE]) for n in ("lg", "eq1", "ca", "lg2", "eq2", "cb"))
        l_max, r1, l_max2, r2 = (sb(n, [P, TILES]) for n in ("l_max", "r1", "l_max2", "r2"))
        hot = sb("hot", [P, TOP, TILES, NE])
        hot_any = sb("hot_any", [P, TILES, NE], BF16)
        rx = sb("rx", [P, TILES, NE + 1])
        rex = sb("rex", [P, TILES, NE + 1])
        den = sb("den", [P, TILES])
        pos = sb("pos", [P, TILES, NE])
        hot_pos = sb("hot_pos", [P, TOP, TILES, NE])
        slot_f = sb("slot_f", [P, TOP, TILES])
        pad_row = sb("pad_row", [P, ROW_W])
        cnt, ng_e, one8, cum = (sb(n, [P, NE]) for n in ("cnt", "ng_e", "one8", "cum"))
        cnt_i, end_i = sb("cnt_i", [P, NE], I32), sb("end_i", [P, NE], I32)
        past = sb("past", [P, NG, NE])
        past_n = sb("past_n", [P, NG, NE])
        grp_e, grp_b, grp_c, grp_r = (sb(n, [P, NG]) for n in ("grp_e", "grp_b", "grp_c", "grp_r"))
        grp_ei, grp_ri = sb("grp_ei", [P, NG], I32), sb("grp_ri", [P, NG], I32)
        g_in = [sb(f"g_in{k}", [P, GT, ROW_W]) for k in range(AHEAD)]
        g_xT = [sb(f"g_xT{q}", [P, 2, GRP], F16) for q in range(2)]
        g_act = [t[:, :, :].rearrange("p t d -> p (t d)").rearrange("p (c r) -> p c r", c=4) for t in (xn, xt)]
        g_h = [t[:, :, :].rearrange("p t d -> p (t d)").bitcast(F16).rearrange("p (h c r) -> p h c r", h=2, c=4)
               for t in (xnT, xtT)] + [sb(f"g_h{k}", [P, 2, 4, GRP], F16)[:, :, :, :] for k in (2, 3)]
        g_y = [sb(f"g_y{k}", [P, GT, D]) for k in range(AHEAD)]
        g_k = sb("g_k", [P, GT])
        g_row = [sb(f"g_row{k}", [P, GT]) for k in range(AHEAD)]
        g_dst = [sb(f"g_dst{k}", [P, GT], U32) for k in range(AHEAD)]

        bank = [ctx.enter_context(nc.psum_tensor(f"bank{k}", [P, 512], F32)) for k in range(8)]
        lg_ps = bank[0][:, 0:TILES * NE]
        rank_ps = bank[7][:, 64:64 + TILES * NE]
        tot_ps = bank[7][:, 128:128 + NE]

        cst_in, vec_in, gw_in, rt_in = sem("cst_in"), sem("vec_in"), sem("gw_in"), sem("rt_in")
        stage_in, stage_used = sem("stage_in"), sem("stage_used")
        set_ready, vecT_ps, vec_ready, set_ps, set_sb, ttl_ps = (
            sem("set_ready"), sem("vecT_ps"), sem("vec_ready"), sem("set_ps"), sem("set_sb"), sem("ttl_ps"))
        dve_chain = sem("dve_chain")
        bw_ps, pool_turns = sem("bw_ps"), sem("pool_turns")
        spare_out = sem("spare_out")
        w_ready = sems("w_ready")
        out_st = sems("out_st")
        fin_done, fin_in = sem("fin_done"), sems("fin_in")

        SL = []
        for L in range(2):
            s = LayerSems(sem, sems, L)
            SL.append(s)

        block = ctx.enter_context(nc.Block())

        def table_values(eng, table, g, n, top):
            at = table[0:1, g:g + n] if isinstance(g, int) else table[0:1, bass.ds(g, n)]
            return nc.values_load_multi_w_load_instructions(at, engines=[eng], min_val=0, max_val=top)[1]
        per = 2
        hid_v = [W1[L].rearrange("e d h -> d e h") for L in range(2)]
        out_v = [W2[L].rearrange("e (c p) d -> p (e c) d", p=P) for L in range(2)]

        @block.sync
        def _(sp):
            sp.dma_start(cst[:, :], consts).then_inc(cst_in, 16)
            rows = [(b1_0.rearrange("e (c p) -> (e c) p", p=P), V_B1[0]), (b1_1.rearrange("e (c p) -> (e c) p", p=P), V_B1[1]),
                    (ln_g, V_G), (ln_b, V_B), (a_src.unsqueeze(0), V_A), (a_dst.unsqueeze(0), V_A + 1),
                    (a_1.rearrange("(k p) o -> k (p o)", p=P), V_A + 2)]
            for src, at in rows:
                sp.dma_start(vec_rows[at:at + src.shape[0], :], src).then_inc(vec_in, 16)
            sp.dma_start(gw[0][:, :], gW0).then_inc(gw_in, 16)
            sp.dma_start(gw[1][:, :], gW1).then_inc(gw_in, 16)
            tok3 = lambda ap, n: ap[bass.ds(n * BLK, BLK), :].rearrange("(t p) w -> p t w", p=P)

            def load_early(L, n, q):
                s = SL[L]
                sp.dma_start(adj_in[q][:, :, :], tok3(adj, n)).then_inc(s.x_in[q], 16)
                if L == 1:
                    for k in range(TOP):
                        sp.dma_start(yin[q][:, k, :, :], y_buf[0][bass.ds(n * BLK + k * N_TOK, BLK), :].rearrange(
                            "(t p) w -> p t w", p=P)).then_inc(s.x_in[q], 16)

            def load_x(L, n, q):
                if L == 0:
                    sp.dma_start(xin[q][:, :, 0:D], tok3(x, n)).then_inc(SL[L].x_in[q], 16)
                else:
                    sp.dma_start(xin[q][:, :, :], tok3(x1_buf[0], n)).then_inc(SL[L].x_in[q], 16)

            def store(L, n, q):
                sp.wait_ge(SL[L].x1w_ready, n + 1)
                sp.dma_start(tok3(x1_buf[L], n), x1w[q][:, :, :]).then_inc(SL[L].stored[q], 16)

            def blocks(L):
                s = SL[L]
                for n in range(2):
                    load_x(L, n, n)
                    load_early(L, n, n)
                if L == 0:
                    for w, b, r, bb in ((wr, br_bc, b2_bc, 0), (wr, br_bc, b2_bc, 1)):
                        sp.dma_start(w[bb][:, :], Wr[bb]).then_inc(rt_in, 16)
                        sp.dma_start(b[bb][:, :], br[bb].unsqueeze(0).to_broadcast([P, NE])).then_inc(rt_in, 16)
                        sp.dma_start(r[bb][:, :, :], b2[bb].unsqueeze(0).to_broadcast([P, NE, D])).then_inc(rt_in, 16)
                stages = [(hid_v[L], NE * HID[L]), (out_v[L], NE * NC[L] * D)]

                def load_stage(m):
                    k = 2 * L + m
                    if k:
                        sp.wait_ge(stage_used, k)
                    src, width = stages[m]
                    sp.dma_start(w_stage[:, 0:width].rearrange("p (a b) -> p a b", a=src.shape[1]), src).then_inc(stage_in, 16)

                def step(i, d):
                    n, q, turn = block_at(i, d)
                    if isinstance(n, int) and n < 0 or not isinstance(n, int) or n + 3 < NBLK:
                        sp.wait_ge(s.taken, n + 2)
                        load_early(L, n + 3, (q + 1) % 2)
                    if not isinstance(n, int) or 0 <= n < NBLK - 2:
                        sp.wait_ge(s.x_done, n + 1)
                        load_x(L, n + 2, q)
                    if not isinstance(n, int) or n >= 1:
                        store(L, n - 1, (q + 1) % 2)
                step(0, -1)
                step(0, 0)
                load_stage(0)
                if L == 0:
                    sp.wait_ge(set_ready, 1)
                    for LL in range(2):
                        sp.dma_start(row_buf[LL][NE * CAP:ROWS, :].rearrange("(t p) w -> p t w", p=P),
                                     pad_row[:, :].unsqueeze(1).to_broadcast([P, SPARE // P, ROW_W])).then_inc(spare_out, 16)
                with sp.Fori(0, (NBLK - 4) // 2) as i:
                    for d in (1, 2):
                        step(i, d)
                for n in range(NBLK - 3, NBLK + 1):
                    step(0, n)
                load_stage(1)

            def groups(L):
                s = SL[L]
                for q in range(2):
                    sp.wait_ge(s.scattered[q], 16 * TOP * TILES * NBLK // 2)
                sp.wait_ge(s.tables, 1)
                for e in range(NE):
                    end = sp.value_load(end_i[0:1, e:e + 1], min_val=0, max_val=NE * CAP - GRP)
                    sp.dma_start(row_buf[L][bass.ds(end, GRP), :].rearrange("(t p) w -> p t w", p=P),
                                 pad_row[:, :].unsqueeze(1).to_broadcast([P, GT, ROW_W])).then_inc(s.pads_out, 16)
                sp.wait_ge(s.pads_out, 16 * NE)
                if L == 0:
                    sp.wait_ge(spare_out, 32)

                def load_group(g, k):
                    r = sp.value_load(grp_ri[0:1, bass.ds(g, 1)], min_val=0, max_val=ROWS - GRP)
                    sp.dma_start(g_in[k][:, :, :], row_buf[L][bass.ds(r, GRP), :].rearrange("(t p) w -> p t w", p=P)
                                 ).then_inc(s.g_loaded[k], 16)
                for k in range(AHEAD):
                    load_group(k, k)
                with sp.Fori(0, TURNS) as i:
                    for k in range(AHEAD):
                        g = AHEAD * i + k
                        sp.wait_ge(s.gT_ps, g + 1)
                        sp.wait_ge(s.placed, g + 1)
                        load_group(g + AHEAD, k)

            def all_written(L):
                for k in range(AHEAD):
                    sp.wait_ge(SL[L].y_out[k], 16 * GT * NG // AHEAD)
                for q in range(2):
                    sp.wait_ge(SL[L].stored[q], 16 * NBLK // 2)

            blocks(0)
            groups(0)
            all_written(0)
            blocks(1)
            groups(1)
            all_written(1)

            def load_last(n, q):
                sp.dma_start(xin[q][:, :, :], tok3(x1_buf[1], n)).then_inc(fin_in[q], 16)
                for k in range(TOP):
                    sp.dma_start(yin[q][:, k, :, :], y_buf[1][bass.ds(n * BLK + k * N_TOK, BLK), :].rearrange(
                        "(t p) w -> p t w", p=P)).then_inc(fin_in[q], 16)

            def store_last(n, q):
                sp.wait_ge(fin_done, n + 1)
                sp.dma_start(tok3(out, n), xin[q][:, :, 0:D]).then_inc(out_st[q], 16)
            for n in range(2):
                load_last(n, n)
            with sp.Fori(0, NBLK // per - 1) as i:
                for q in range(2):
                    n = per * i + q
                    store_last(n, q)
                    sp.wait_ge(out_st[q], 16 * (i + 1))
                    load_last(n + per, q)
            for q in range(2):
                store_last(NBLK - per + q, q)
            for q in range(2):
                sp.wait_ge(out_st[q], 16 * NBLK // 2)

        @block.gpsimd
        def _(pool):
            for L in range(2):
                s = SL[L]
                with pool.Fori(0, NBLK // per) as i:
                    for q in range(2):
                        pool.wait_ge(s.slots_ready, per * i + q + 1)
                        pool.sem_inc(pool_turns, 1)
                        for k in range(TOP):
                            for t in range(TILES):
                                pool.indirect_dma_start(
                                    row_buf[L][:, :], bass.IndirectOffsetOnAxis(ap=slot[q][:, k, t:t + 1], axis=0),
                                    pay[q][:, t, :], None).then_inc(s.scattered[q], 16)
                with pool.Fori(0, NG // AHEAD) as i:
                    for k in range(AHEAD):
                        pool.wait_ge(s.y_ready, AHEAD * i + k + 1)
                        pool.sem_inc(pool_turns, 1)
                        for t in range(GT):
                            pool.indirect_dma_start(
                                y_buf[L][:, :], bass.IndirectOffsetOnAxis(ap=g_dst[k][:, t:t + 1], axis=0),
                                g_y[k][:, t, :], None, bounds_check=TOP * N_TOK - 1, oob_is_err=False
                            ).then_inc(s.y_out[k], 16)

        @block.tensor
        def _(pe):
            pe.wait_ge(vec_in, 16 * 7)
            pe.wait_ge(cst_in, 16)
            nc.tensor.transpose(bank[0][:, 0:68], vec_rows[:, :], ident[0:68, 0:68]).then_inc(vecT_ps, 1)
            pe.wait_ge(gw_in, 32)
            for L in range(2):
                last = nc.tensor.transpose(bank[1][:, L * P:(L + 1) * P], gw[L][:, :], ident)
            last.then_inc(set_ps, 1)
            pe.wait_ge(vec_ready, 1)
            for k in range(4):
                lhsT = gw[0] if k < 2 else gwT[1]
                last = nc.tensor.matmul(bank[2][:, k * NODES:(k + 1) * NODES], lhsT[:, :], att_vec[:, k, :],
                                        start=True, stop=True)
            last.then_inc(ttl_ps, 1)
            pe.wait_ge(set_sb, 1)
            pe.wait_ge(rt_in, 16 * 6)

            def transpose_tiles(src):
                for t in range(TILES):
                    last = nc.tensor.transpose(bank[t // 4][:, (t % 4) * P:(t % 4 + 1) * P], src[:, t, :], ident)
                return last

            def transpose_input(L, n):
                pe.wait_ge(SL[L].xn_ready, n + 1)
                transpose_tiles(xn).then_inc(SL[L].xT_ps, 1)

            def features(L, n):
                s = SL[L]
                w_h = gwT[0] if L == 0 else gw[1]
                pe.wait_ge(s.xT_sb, n + 1)
                halves = xnT[:, :, :].rearrange("p t (g j) -> p t g j", g=2)
                for g in range(2):
                    nc.tensor.matmul(bank[2][g * NODES:(g + 1) * NODES, :], to_score[:, 2 * L + 1, :], halves[:, :, g, :],
                                     start=True, stop=False, skip_group_check=True)
                for t in range(TILES):
                    last = nc.tensor.matmul(bank[2][:, t * NODES:(t + 1) * NODES], xnT[:, t, :], to_score[:, 2 * L, :],
                                            start=False, stop=(t == TILES - 1), skip_group_check=True)
                last.then_inc(s.e_ps, 1)
                for t in range(TILES):
                    last = nc.tensor.matmul(bank[3 + t // 4][:, (t % 4) * P:(t % 4 + 1) * P], xnT[:, t, :], w_h[:, :],
                                            start=True, stop=True)
                last.then_inc(s.hs_ps, 1)

            def attention(L, n):
                s = SL[L]
                pe.wait_ge(s.E_sb, n + 1)
                transpose_tiles(pair_e).then_inc(s.ET_ps, 1)
                pe.wait_ge(s.hs_sb, n + 1)
                pe.wait_ge(s.ET_sb, n + 1)
                for t in range(TILES):
                    last = nc.tensor.matmul(bank[5 + t // 4][:, (t % 4) * P:(t % 4 + 1) * P], pair_eT[:, t, :], h_sb[:, t, :],
                                            start=True, stop=True)
                last.then_inc(s.att_ps, 1)

            def ranks(L, n):
                s = SL[L]
                pe.wait_ge(s.hot_ready, n + 1)
                hot_v = hot_any[:, :, :].rearrange("p t e -> p (t e)")
                nc.tensor.matmul(rank_ps, tri16[:, :], hot_v, start=True, stop=False, skip_group_check=True)
                for d in range(1, TILES):
                    nc.tensor.matmul(rank_ps[:, d * NE:], ones16[:, :], hot_v[:, 0:(TILES - d) * NE],
                                     start=False, stop=(d == TILES - 1), skip_group_check=True)
                for t in range(TILES):
                    last = nc.tensor.matmul(tot_ps, ones16[:, :], hot_v[:, t * NE:(t + 1) * NE],
                                            start=(t == 0), stop=(t == TILES - 1), skip_group_check=True)
                last.then_inc(s.rank_done, 1)

            def logits(L, n):
                s = SL[L]
                pe.wait_ge(s.xt_ready, n + 1)
                transpose_tiles(xt).then_inc(s.xtT_ps, 1)
                pe.wait_ge(s.xtT_sb, n + 1)
                for t in range(TILES):
                    last = nc.tensor.matmul(lg_ps[:, t * NE:(t + 1) * NE], xtT[:, t, :], wr[L][:, :], start=True, stop=True)
                last.then_inc(s.lg_done, 1)

            def blocks(L):
                def step(n, first=False, last=False):
                    attention(L, n)
                    if not last:
                        transpose_input(L, n + 1)
                    if not first:
                        ranks(L, n - 1)
                    if not last:
                        features(L, n + 1)
                    logits(L, n)
                transpose_input(L, 0)
                features(L, 0)
                step(0, first=True)
                with pe.Fori(0, NBLK // per - 1) as i:
                    for d in (1, 2):
                        step(per * i + d)
                step(NBLK - 1, last=True)
                ranks(L, NBLK - 1)

            def groups(L):
                s = SL[L]
                x_ps = [bank[b][:, 0:GRP].bitcast(F16).rearrange("p (h n) -> p h n", h=2) for b in (4, 7)]

                def to_feature_rows(k, turn):
                    q, turn = k % 2, turn + k // AHEAD
                    pe.wait_ge(s.g_loaded[k % AHEAD], 16 * (turn + 1))
                    rows16 = g_in[k % AHEAD][:, :, :].bitcast(F16)
                    for hl in range(2):
                        for t in range(GT):
                            last = nc.tensor.transpose(x_ps[q][:, hl, t * P:(t + 1) * P],
                                                       rows16[:, t, hl * D:(hl + 1) * D], ident16[:, :])
                    last.then_inc(s.gT_ps, 1)

                def experts(g, n):
                    return table_values(mybir.EngineType.PE, grp_ei, g, n, NE - 1)

                def up(g, q, e):
                    wait_past(pe, s.act_done, (g - 1) * NC[L])
                    pe.wait_ge(s.gT_sb, g + 1)
                    w = w1[L][:, :, :, :].rearrange("p e a h -> p (e a h)")
                    for c in range(NC[L]):
                        dst = bank[2 * q + c // 2][:, (c % 2) * GRP:(c % 2 + 1) * GRP]
                        for m, (wp, xp) in enumerate(((0, 0), (0, 1), (1, 0))):
                            last = nc.tensor.matmul(dst, w[:, bass.ds(e * (2 * HID[L]) + (wp * HID[L] + c * P), P)],
                                                    g_xT[q][:, xp, :], start=(m == 0), stop=(m == 2))
                        if c % 2:
                            last.then_inc(s.h_ps, 1)

                def down(g, k, e):
                    w = w2[L][:, :, :, :, :].rearrange("p e c a d -> p (e c a d)")
                    wait_past(pe, s.y_ready, g - 1)
                    pe.wait_ge(s.h_split, (NC[L] // 2) * (g + 1))
                    for t in range(GT):
                        m = 0
                        for c in range(NC[L]):
                            for wp, hp in ((0, 0), (0, 1), (1, 0)):
                                last = nc.tensor.matmul(
                                    bank[5 + k % 2][:, t * D:(t + 1) * D], g_h[k][:, hp, c, t * P:(t + 1) * P],
                                    w[:, bass.ds(e * (2 * HID[L]) + (2 * c + wp) * D, D)],
                                    start=(m == 0), stop=(m == 3 * NC[L] - 1))
                                m += 1
                    last.then_inc(s.y_done, 1)

                pe.wait_ge(s.tables, 1)
                pe.wait_ge(w_ready[L], 1)
                for k in range(2):
                    to_feature_rows(k, 0)
                es = experts(0, 2)
                up(0, 0, es[0])
                to_feature_rows(2, 0)
                up(1, 1, es[1])

                def turn(i, last=False):
                    es = experts(AHEAD * i, AHEAD if last else AHEAD + 2)
                    for k in range(AHEAD):
                        g = AHEAD * i + k
                        if not last or k + 3 < AHEAD:
                            to_feature_rows(k + 3, i)
                        if not last or k + 2 < AHEAD:
                            up(g + 2, k % 2, es[k + 2])
                        down(g, k, es[k])
                turn(0)
                with pe.Fori(1, TURNS) as i:
                    turn(i)
                turn(TURNS, last=True)

            for L in range(2):
                blocks(L)
                if L == 0:
                    pe.wait_ge(stage_in, 16)
                    for e in range(NE):
                        for c in range(NC[0]):
                            k = e * NC[0] + c
                            last = nc.tensor.matmul(bank[0][:, k:k + 1], w_stage[:, e * HID[0] + c * P:e * HID[0] + (c + 1) * P],
                                                    vec_cols[:, V_B + e:V_B + e + 1], start=True, stop=True)
                    last.then_inc(bw_ps, 1)
                groups(L)

        @block.scalar
        def _(act):
            act.wait_ge(set_sb, 1)

            def copy_banks(b, dst, func=ACT.Copy):
                for k in range(2):
                    last = nc.scalar.activation(dst[:, 4 * k:4 * k + 4, :], bank[b + k][:, :].rearrange("p (t d) -> p t d", d=P),
                                                func)
                return last

            def normalise(dst, src, rstd, nmr, at):
                for t in range(TILES):
                    last = nc.scalar.activation(dst[:, t, :], src[:, t, :], ACT.Identity, bias=nmr[:, at + t:at + t + 1],
                                                scale=rstd[:, at + t:at + t + 1])
                return last

            def norm_input(L, n, q):
                act.wait_ge(SL[L].st1, n + 1)
                normalise(xn, xin[q][:, :, 0:D], rstd1, nmr1, 0).then_inc(SL[L].xn_ready, 1)

            def attention(L, n):
                s = SL[L]
                act.wait_ge(s.e_ready, n + 1)
                for g in range(2):
                    r = slice(g * NODES, (g + 1) * NODES)
                    last = nc.scalar.activation(pair_e[r, :, r], e_dif[r, :].rearrange("p (t j) -> p t j", j=NODES), ACT.Exp)
                last.then_inc(s.E_sb, 1)
                act.wait_ge(s.ET_ps, n + 1)
                copy_banks(0, pair_eT).then_inc(s.ET_sb, 1)

            def input_columns(L, n):
                act.wait_ge(SL[L].xT_ps, n + 1)
                copy_banks(0, xnT).then_inc(SL[L].xT_sb, 1)

            def features(L, n):
                s = SL[L]
                act.wait_ge(s.e_ps, n + 1)
                nc.scalar.activation(e_sb[:, :], bank[2][:, :], ACT.Copy).then_inc(s.e_copied, 1)
                act.wait_ge(s.hs_ps, n + 1)
                copy_banks(3, h_sb).then_inc(s.hs_sb, 1)

            def expert_norm(L, n):
                act.wait_ge(SL[L].st1, n + 3)
                normalise(xff, xt, rstd1, nmr1, TILES).then_inc(SL[L].ff_ready, 1)

            def high_parts(L, n, q, turn):
                s = SL[L]
                if L == 0:
                    act.wait_ge(s.ff_ready, n + 1)
                wait_past(act, s.scattered[q], 16 * TOP * TILES * turn)
                nc.scalar.activation(pay[q][:, :, :].bitcast(F16)[:, :, 0:D], (xff if L == 0 else xt)[:, :, :],
                                     ACT.Copy, scale=S_X).then_inc(s.hi_ready, 1)

            def router(L, n):
                act.wait_ge(SL[L].hot_ready, n + 1)
                nc.scalar.activation(rex[:, :, :], rx[:, :, :], ACT.Exp).then_inc(SL[L].rexp, 1)

            def blocks(L):
                s = SL[L]

                def step(i, d, first=False, last=False):
                    n, q, turn = block_at(i, d)
                    attention(L, n)
                    if not last:
                        norm_input(L, n + 1, (q + 1) % 2)
                    if L == 1:
                        act.wait_ge(s.att_ps, n + 1)
                        copy_banks(5, h_new, ACT.Relu).then_inc(s.att_sb, 1)
                    if not last:
                        input_columns(L, n + 1)
                    if not first:
                        router(L, n - 1)
                        if L == 0:
                            expert_norm(L, n - 1)
                    if not last:
                        features(L, n + 1)
                    if not first:
                        high_parts(L, *block_at(i, d - 1))
                    act.wait_ge(s.st2, n + 1)
                    wait_past(act, s.hi_ready, n)
                    normalise(xt, x1w[q][:, :, 0:D], rstd2, nmr2, 0).then_inc(s.xt_ready, 1)
                    act.wait_ge(s.xtT_ps, n + 1)
                    copy_banks(0, xtT).then_inc(s.xtT_sb, 1)
                    act.wait_ge(s.lg_done, n + 1)
                    nc.scalar.activation(lg_raw[:, :, :], lg_ps.rearrange("p (t e) -> p t e", e=NE), ACT.Copy).then_inc(s.lg_copied, 1)
                norm_input(L, 0, 0)
                input_columns(L, 0)
                features(L, 0)
                step(0, 0, first=True)
                with act.Fori(0, NBLK // per - 1) as i:
                    for d in (1, 2):
                        step(i, d)
                step(0, NBLK - 1, last=True)
                router(L, NBLK - 1)
                if L == 0:
                    expert_norm(L, NBLK - 1)
                high_parts(L, *block_at(0, NBLK - 1))

            def groups(L):
                s = SL[L]
                x_ps = [bank[b][:, 0:GRP].bitcast(F16).rearrange("p (h n) -> p h n", h=2) for b in (4, 7)]

                def copy_x(g, q):
                    act.wait_ge(s.gT_ps, g + 1)
                    nc.scalar.activation(g_xT[q][:, :, :], x_ps[q], ACT.Copy).then_inc(s.gT_sb, 1)

                def gelu(g, q, e):
                    wait_past(act, s.h_split, (g - 1) * (NC[L] // 2))
                    for c in range(NC[L]):
                        if c % 2 == 0:
                            act.wait_ge(s.h_ps, NC[L] // 2 * g + c // 2 + 1)
                        nc.scalar.activation(g_act[q][:, c, :], bank[2 * q + c // 2][:, (c % 2) * GRP:(c % 2 + 1) * GRP],
                                             ACT.Gelu, bias=b1_cols[L][:, bass.ds(e * NC[L] + c, 1)],
                                             scale=1.0 / (S_X * S_W)).then_inc(s.act_done, 1)

                def experts(g, n):
                    return table_values(mybir.EngineType.Activation, grp_ei, g, n, NE - 1)
                act.wait_ge(s.tables, 1)
                act.wait_ge(w_ready[L], 1)
                for k in range(2):
                    copy_x(k, k)
                es = experts(0, 2)
                gelu(0, 0, es[0])
                copy_x(2, 0)
                gelu(1, 1, es[1])

                def turn(i, last=False):
                    n = 2 if last else AHEAD
                    es = experts(AHEAD * i + 2, n)
                    for k in range(n):
                        if not last or k == 0:
                            copy_x(AHEAD * i + k + 3, (k + 1) % 2)
                        gelu(AHEAD * i + k + 2, k % 2, es[k])
                with act.Fori(0, TURNS) as i:
                    turn(i)
                turn(TURNS, last=True)

            for L in range(2):
                blocks(L)
                groups(L)

        @block.vector
        def _(dve):
            ch = Chain(dve, dve_chain)
            V = nc.vector
            V.memset(ones16[:, :], 1.0)
            V.memset(one8[:, :], 1.0)
            V.memset(pair_e[:, :, :], 0.0)
            ch.did(V.memset(pad_row[:, :], 0.0))
            ch.wait()
            V.memset(pad_row[:, D:D + 1], float(NO_TOKEN)).then_inc(set_ready, 1)
            dve.wait_ge(cst_in, 16)
            V.tensor_copy(ident16[:, :], ident)
            V.tensor_copy(tri16[:, :], cst[:, C_TRI:C_TRI + P])
            V.tensor_copy(tok_run[:, :], cst[:, C_TOK:C_TOK + TILES])
            for L in range(2):
                V.tensor_copy(base_run[L][:, :], cst[:, C_BASE:C_BASE + NE])
            dve.wait_ge(vecT_ps, 1)
            ch.did(V.tensor_copy(vec_cols[:, :], bank[0][:, 0:68]))
            ch.wait()
            V.tensor_scalar(gain[:, :], vec_cols[:, V_G:V_G + NE], S_W, None, ALU.mult)
            V.tensor_copy(b1_cols[1][:, :], vec_cols[:, V_B1[1]:V_B1[1] + NE * NC[1]])
            V.tensor_copy(att_vec[:, :, :], vec_cols[:, V_A:V_A + 4].unsqueeze(2).to_broadcast([P, 4, NODES]))
            dve.wait_ge(set_ps, 1)
            V.tensor_copy(gwT[0][:, :], bank[1][:, 0:P])
            V.tensor_copy(gwT[1][:, :], bank[1][:, P:2 * P]).then_inc(vec_ready, 1)
            dve.wait_ge(ttl_ps, 1)
            V.tensor_copy(to_score[:, :, :], bank[2][:, 0:4 * NODES].rearrange("p (k j) -> p k j", j=NODES)).then_inc(set_sb, 1)
            dve.wait_ge(set_sb, 1)
            dve.wait_ge(rt_in, 16 * 6)

            rev = cst[:, C_REV:C_REV + TILES * NE].rearrange("p (t e) -> p t e", e=NE)
            bc = lambda ap: ap.unsqueeze(2).to_broadcast([P, TILES, NE])

            def statistics(srcs, rstd, nmr):
                W = TILES * len(srcs)
                for m, src in enumerate(srcs):
                    for t in range(TILES):
                        last = V.bn_stats(stat[:, m * TILES + t, :], src[:, t, :])
                ch.did(last)
                ch.wait()
                w = slice(0, W)
                V.tensor_tensor(msum[:, w], stat[:, w, 1], stat[:, w, 4], ALU.add)
                V.tensor_tensor(m2s[:, w], stat[:, w, 2], stat[:, w, 5], ALU.add)
                ch.did(V.tensor_tensor(mdif[:, w], stat[:, w, 1], stat[:, w, 4], ALU.subtract))
                ch.wait()
                V.tensor_scalar(mean[:, w], msum[:, w], -0.5, None, ALU.mult)
                ch.did(V.tensor_tensor(mdif2[:, w], mdif[:, w], mdif[:, w], ALU.mult))
                ch.wait()
                ch.did(V.scalar_tensor_tensor(var[:, w], mdif2[:, w], D / 4.0, m2s[:, w], ALU.mult, ALU.add))
                ch.wait()
                ch.did(V.tensor_scalar(ve[:, w], var[:, w], 1.0 / D, EPS, ALU.mult, ALU.add))
                ch.wait()
                ch.did(V.tensor_scalar(half_bits[:, w], ve[:, w].bitcast(I32), 1, None, ALU.logical_shift_right))
                ch.wait()
                y = [nt1[:, w], nt3[:, w]]
                ch.did(V.tensor_scalar(y[0].bitcast(I32), half_bits[:, w], -1.0, float(0x5f3759df), ALU.mult, ALU.add))
                for k in range(3):
                    ch.wait()
                    ch.did(V.tensor_tensor(nt2[:, w], y[0], y[0], ALU.mult))
                    ch.wait()
                    ch.did(V.scalar_tensor_tensor(nt2[:, w], nt2[:, w], -0.5, ve[:, w], ALU.mult, ALU.mult))
                    ch.wait()
                    out_y = y[1] if k < 2 else rstd[:, w]
                    ch.did(V.scalar_tensor_tensor(out_y, nt2[:, w], 1.5, y[0], ALU.add, ALU.mult))
                    y.reverse()
                ch.wait()
                return V.tensor_tensor(nmr[:, w], mean[:, w], rstd[:, w], ALU.mult)

            def add_experts(src, y):
                for k in range(TOP):
                    for t in range(TILES):
                        last = V.scalar_tensor_tensor(src[:, t, 0:D], y[:, k, t, :], src[:, t, D + k:D + k + 1],
                                                      src[:, t, 0:D], ALU.mult, ALU.add)
                    if k == 0:
                        ch.did(last)
                        ch.wait()
                return last

            def scores(L, n):
                s = SL[L]
                dve.wait_ge(s.e_copied, n + 1)
                ch.did(V.scalar_tensor_tensor(e_act[:, :], e_sb[:, :], 0.2, e_sb[:, :], ALU.mult, ALU.max))
                ch.wait()
                ch.did(V.scalar_tensor_tensor(e_msk[:, :], keep[:, :], MASKED[L], e_act[:, :], ALU.add, ALU.min))
                ch.wait()
                e3 = e_msk[:, :].rearrange("p (t j) -> p t j", j=NODES)
                ch.did(V.tensor_reduce(e_max[:, :], e3, AX_X, ALU.max))
                ch.wait()
                V.tensor_tensor(e_dif[:, :].rearrange("p (t j) -> p t j", j=NODES), e3,
                                e_max[:, :].unsqueeze(2).to_broadcast([P, TILES, NODES]), ALU.subtract).then_inc(s.e_ready, 1)

            def take_in(L, n, q, turn):
                s = SL[L]
                dve.wait_ge(s.x_in[q], (32 if L == 0 else 64) * (turn + 1))
                if L == 1:
                    ch.did(add_experts(xin[q], yin[q]))
                    ch.wait()
                V.tensor_scalar(keep[:, :], adj_in[q][:, :, :].rearrange("p t j -> p (t j)"), 0.0, BIG,
                                ALU.not_equal if L == 0 else ALU.is_gt, ALU.mult).then_inc(s.taken, 1)

            def add_attention(L, n, q, turn):
                s = SL[L]
                dve.wait_ge(s.E_sb, n + 1)
                ch.did(V.tensor_reduce(sum_sb[:, :], pair_e[:, :, :], AX_X, ALU.add))
                ch.wait()
                ch.did(V.reciprocal(rinv[:, :], sum_sb[:, :]))
                dve.wait_ge(s.att_ps if L == 0 else s.att_sb, n + 1)
                wait_past(dve, s.stored[q], 16 * turn)
                ch.wait()
                for t in range(TILES):
                    att = bank[5 + t // 4][:, (t % 4) * P:(t % 4 + 1) * P] if L == 0 else h_new[:, t, :]
                    last = V.scalar_tensor_tensor(x1w[q][:, t, 0:D], att, rinv[:, t:t + 1], xin[q][:, t, 0:D], ALU.mult, ALU.add)
                last.then_inc(s.x_done, 1)
                dve.wait_ge(s.x_done, n + 1)
                statistics([x1w[q][:, :, 0:D]], rstd2, nmr2).then_inc(s.st2, 1)

            def route(L, n, q, turn):
                s = SL[L]
                dve.wait_ge(s.lg_copied, n + 1)
                wait_past(dve, s.scattered[q], 16 * TOP * TILES * turn)
                ch.did(V.tensor_tensor(lg[:, :, :], lg_raw[:, :, :],
                                       br_bc[L][:, :].unsqueeze(1).to_broadcast([P, TILES, NE]), ALU.add))
                V.tensor_copy(pay[q][:, :, D], tok_run[:, :])

                def first_max(val, vmax, eq, cand, cmax, k):
                    ch.wait()
                    ch.did(V.tensor_reduce(vmax[:, :], val[:, :, :], AX_X, ALU.max))
                    ch.wait()
                    ch.did(V.tensor_tensor(eq[:, :, :], val[:, :, :], bc(vmax[:, :]), ALU.is_equal))
                    ch.wait()
                    ch.did(V.tensor_tensor(cand[:, :, :], eq[:, :, :], rev, ALU.mult))
                    ch.wait()
                    ch.did(V.tensor_reduce(cmax[:, :], cand[:, :, :], AX_X, ALU.max))
                    ch.wait()
                    ch.did(V.tensor_tensor(hot[:, k, :, :], cand[:, :, :], bc(cmax[:, :]), ALU.is_equal))
                first_max(lg, l_max, eq1, ca, r1, 0)
                ch.wait()
                V.tensor_scalar(tok_run[:, :], tok_run[:, :], float(BLK), None, ALU.add)
                V.tensor_scalar(pay[q][:, :, D + 1], r1[:, :], -1.0, float(NE), ALU.mult, ALU.add)
                V.tensor_tensor(rx[:, :, 0:NE], lg[:, :, :], bc(l_max[:, :]), ALU.subtract)
                ch.did(V.scalar_tensor_tensor(lg2[:, :, :], hot[:, 0, :, :], -BIG, lg[:, :, :], ALU.mult, ALU.add))
                first_max(lg2, l_max2, eq2, cb, r2, 1)
                ch.wait()
                V.tensor_tensor(rx[:, :, NE], l_max2[:, :], l_max[:, :], ALU.subtract)
                V.tensor_tensor(hot_any[:, :, :], hot[:, 0, :, :], hot[:, 1, :, :], ALU.add).then_inc(s.hot_ready, 1)

            def low_parts(L, n, q):
                ff, pay16 = (xff if L == 0 else xt), pay[q][:, :, :].bitcast(F16)
                dve.wait_ge(SL[L].hi_ready, n + 1)
                ch.did(V.scalar_tensor_tensor(pay16[:, :, D:2 * D], ff[:, :, :], S_X, pay16[:, :, 0:D], ALU.mult, ALU.subtract))

            def places(L, n, q):
                s = SL[L]
                dve.wait_ge(s.rank_done, n + 1)
                ch.did(V.tensor_tensor(pos[:, :, :], rank_ps.rearrange("p (t e) -> p t e", e=NE),
                                       base_run[L][:, :].unsqueeze(1).to_broadcast([P, TILES, NE]), ALU.add))
                dve.wait_ge(s.rexp, n + 1)
                if L == 0:
                    ch.did(V.tensor_scalar(den[:, :], rex[:, :, NE], 1.0, None, ALU.add))
                else:
                    ch.did(V.tensor_reduce(den[:, :], rex[:, :, 0:NE], AX_X, ALU.add))
                ch.wait()
                V.tensor_tensor(base_run[L][:, :], base_run[L][:, :], tot_ps, ALU.add)
                for k in range(TOP):
                    V.tensor_tensor(hot_pos[:, k, :, :], hot[:, k, :, :], pos[:, :, :], ALU.mult)
                ch.did(V.reciprocal(x1w[q][:, :, D], den[:, :]))
                ch.wait()
                V.tensor_tensor(x1w[q][:, :, D + 1], x1w[q][:, :, D], rex[:, :, NE], ALU.mult).then_inc(s.x1w_ready, 1)
                ch.did(V.tensor_reduce(slot_f[:, :, :], hot_pos[:, :, :, :], AX_X, ALU.add))
                ch.wait()
                V.tensor_copy(slot[q][:, :, :], slot_f[:, :, :]).then_inc(s.slots_ready, 1)

            def blocks(L):
                s = SL[L]

                def statistics_of(n, q, has_input, has_ff):
                    srcs = [xin[q][:, :, 0:D]] if has_input else []
                    if has_ff:
                        dve.wait_ge(s.xt_ready, n - 1)
                        srcs.append(xt)
                    at = 0 if has_input else TILES
                    if srcs:
                        statistics(srcs, rstd1[:, at:], nmr1[:, at:]).then_inc(s.st1, 1)

                def step(i, d):
                    n, q, turn = block_at(i, d)
                    first, last, over = ((n == 0, n == NBLK - 1, n == NBLK) if isinstance(n, int) else (False, False, False))
                    if not over:
                        scores(L, n)
                    if not (last or over):
                        take_in(L, *block_at(i, d + 1))
                    statistics_of(n + 1, (q + 1) % 2, not (last or over), L == 0 and not first)
                    if not first:
                        route(L, *block_at(i, d - 1))
                        if L == 1 or over:
                            low_parts(L, n - 1, (q + 1) % 2)
                    if not over:
                        add_attention(L, n, q, turn)
                    if not first:
                        if L == 0 and not over:
                            low_parts(L, n - 1, (q + 1) % 2)
                        places(L, n - 1, (q + 1) % 2)
                take_in(L, 0, 0, 0)
                statistics_of(0, 0, True, False)
                step(0, 0)
                with dve.Fori(0, NBLK // per - 1) as i:
                    ch.loop(i, 0, DVE_SIGNALS[L])
                    for d in (1, 2):
                        step(i, d)
                ch.looped(NBLK // per - 1, DVE_SIGNALS[L])
                step(0, NBLK - 1)
                step(0, NBLK)

            def group_tables(L):
                s = SL[L]
                dve.wait_ge(s.slots_ready, NBLK)
                base0 = cst[:, C_BASE:C_BASE + NE]
                V.tensor_copy(end_i[:, :], base_run[L][:, :])
                ch.did(V.tensor_tensor(cnt[:, :], base_run[L][:, :], base0, ALU.subtract))
                ch.wait()
                ch.did(V.tensor_scalar(cnt_i[:, :], cnt[:, :], float(GRP - 1), None, ALU.add))
                ch.wait()
                ch.did(V.tensor_scalar(cnt_i[:, :], cnt_i[:, :], 8, None, ALU.logical_shift_right))
                ch.wait()
                ch.did(V.tensor_copy(ng_e[:, :], cnt_i[:, :]))
                ch.wait()
                ch.did(V.tensor_tensor_scan(cum[:, :], one8[:, :], ng_e[:, :], 0.0, ALU.mult, ALU.add))
                ch.wait()
                g_no = cst[:, C_G:C_G + NG]
                wide = [P, NG, NE]
                ch.did(V.tensor_tensor(past[:, :, :], cum[:, :].unsqueeze(1).to_broadcast(wide),
                                       g_no.unsqueeze(2).to_broadcast(wide), ALU.is_le))
                ch.wait()
                V.tensor_reduce(grp_e[:, :], past[:, :, :], AX_X, ALU.add)
                ch.did(V.tensor_tensor(past_n[:, :, :], past[:, :, :], ng_e[:, :].unsqueeze(1).to_broadcast(wide), ALU.mult))
                ch.wait()
                ch.did(V.tensor_reduce(grp_b[:, :], past_n[:, :, :], AX_X, ALU.add))
                ch.wait()
                V.tensor_scalar(grp_r[:, :], grp_e[:, :], float(CAP), None, ALU.mult)
                ch.did(V.tensor_tensor(grp_c[:, :], g_no, grp_b[:, :], ALU.subtract))
                ch.wait()
                V.tensor_scalar(grp_ei[:, :], grp_e[:, :], float(NE - 1), None, ALU.min)
                ch.did(V.scalar_tensor_tensor(grp_b[:, :], grp_c[:, :], float(GRP), grp_r[:, :], ALU.mult, ALU.add))
                ch.wait()
                V.tensor_copy(grp_ri[:, :], grp_b[:, :]).then_inc(s.tables, 1)

            def split_weights(L):
                dve.wait_ge(stage_in, 16 * (2 * L + 1))
                if L == 0:
                    dve.wait_ge(bw_ps, 1)
                    V.tensor_tensor(b1_cols[0][:, :], bank[0][:, 0:NE * NC[0]], vec_cols[:, 0:NE * NC[0]], ALU.add)
                for part in range(2):
                    for e in range(NE):
                        st = w_stage[:, e * HID[L]:(e + 1) * HID[L]]
                        scale = gain[:, e:e + 1] if L == 0 else S_W
                        if part == 0:
                            last = V.tensor_scalar(w1[L][:, e, 0, :], st, scale, None, ALU.mult)
                        else:
                            last = V.scalar_tensor_tensor(w1[L][:, e, 1, :], st, scale, w1[L][:, e, 0, :], ALU.mult, ALU.subtract)
                    if part == 0:
                        ch.did(last)
                        ch.wait()
                last.then_inc(stage_used, 1)
                dve.wait_ge(stage_in, 16 * (2 * L + 2))
                st = w_stage[:, 0:NE * NC[L] * D].rearrange("p (ec d) -> p ec d", d=D)
                hi, lo = (w2[L][:, :, :, k, :].rearrange("p e c d -> p (e c) d") for k in range(2))
                ch.did(V.tensor_scalar(hi, st, S_W, None, ALU.mult))
                ch.wait()
                V.scalar_tensor_tensor(lo, st, S_W, hi, ALU.mult, ALU.subtract).then_inc(w_ready[L], 1)
                dve.wait_ge(w_ready[L], 1)
                V.memset(g_k[:, :], 0.0).then_inc(stage_used, 1)
                dve.wait_ge(stage_used, 2 * (L + 1))

            def groups(L):
                s = SL[L]
                half = NC[L] // 2

                def place(g, k, turn):
                    dve.wait_ge(s.g_loaded[k], 16 * (turn + 1))
                    wait_past(dve, s.placed, g)
                    ch.did(V.tensor_scalar(g_k[:, :], g_in[k][:, :, D + 1], grp_e[:, bass.ds(g, 1)], float(N_TOK),
                                           ALU.not_equal, ALU.mult))
                    ch.wait()
                    V.tensor_tensor(g_row[k][:, :], g_k[:, :], g_in[k][:, :, D], ALU.add).then_inc(s.placed, 1)

                def split(g, k):
                    part = [slice(2 * hf, 2 * hf + 2) for hf in range(half)]
                    a = g_act[k % 2]
                    for hf in range(half):
                        dve.wait_ge(s.act_done, NC[L] * g + 2 * hf + 2)
                        ch.did(V.tensor_scalar(g_h[k][:, 0, part[hf], :], a[:, part[hf], :], S_H, None, ALU.mult))
                    for hf in range(half):
                        if hf == 0:
                            ch.wait()
                        V.scalar_tensor_tensor(g_h[k][:, 1, part[hf], :], a[:, part[hf], :], S_H,
                                               g_h[k][:, 0, part[hf], :], ALU.mult, ALU.subtract).then_inc(s.h_split, 1)

                def experts(g, n):
                    return table_values(mybir.EngineType.DVE, grp_ei, g, n, NE - 1)

                def finish(g, k, turn, e):
                    wait_past(dve, s.y_out[k], 16 * GT * turn)
                    dve.wait_ge(s.placed, g + 1)
                    V.tensor_copy(g_dst[k][:, :], g_row[k][:, :])
                    dve.wait_ge(s.y_done, g + 1)
                    flat = b2_bc[L][:, :, :].rearrange("p e d -> p (e d)")
                    V.scalar_tensor_tensor(g_y[k][:, :, :], bank[5 + k % 2][:, 0:GT * D].rearrange("p (t d) -> p t d", d=D),
                                           1.0 / (S_H * S_W), flat[:, bass.ds(e * D, D)].unsqueeze(1).to_broadcast([P, GT, D]),
                                           ALU.mult, ALU.add).then_inc(s.y_ready, 1)
                for k in range(2):
                    place(k, k, 0)
                    split(k, k)
                turn_signals = AHEAD * (half + 1)

                def turn(i, last=False):
                    es = experts(AHEAD * i, AHEAD)
                    for k in range(AHEAD):
                        g, a = AHEAD * i + k, (k + 2) % AHEAD
                        if not last or k + 2 < AHEAD:
                            place(g + 2, a, i + (k + 2) // AHEAD)
                            split(g + 2, a)
                        finish(g, k, i, es[k])
                turn(0)
                with dve.Fori(1, TURNS) as i:
                    ch.loop(i, 1, turn_signals)
                    turn(i)
                ch.looped(TURNS - 1, turn_signals)
                turn(TURNS, last=True)

            for L in range(2):
                blocks(L)
                if L == 0:
                    ch.did(V.tensor_copy(tok_run[:, :], cst[:, C_TOK:C_TOK + TILES]))
                group_tables(L)
                split_weights(L)
                groups(L)
            with dve.Fori(0, NBLK // per) as i:
                ch.loop(i, 0, 2)
                for q in range(2):
                    dve.wait_ge(fin_in[q], 48 * (i + 1))
                    add_experts(xin[q], yin[q]).then_inc(fin_done, 1)
            ch.looped(NBLK // per, 2)


_INS = ['x', 'adj', 'L0_gnn_W', 'L0_gnn_a_src', 'L0_gnn_a_dst', 'L0_ffn_Wr', 'L0_ffn_br', 'L0_ffn_ln_g', 'L0_ffn_ln_b',
        'L0_ffn_W1', 'L0_ffn_b1', 'L0_ffn_W2', 'L0_ffn_b2', 'L1_gnn_W', 'L1_gnn_a', 'L1_ffn_gate_w', 'L1_ffn_gate_b',
        'L1_ffn_W1', 'L1_ffn_b1', 'L1_ffn_W2', 'L1_ffn_b2']


def kernel(**inputs):
    import numpy as _np
    import concourse.bacc as _bacc
    from concourse import mybir as _mybir
    from concourse.bass_utils import run_bass_kernel_spmd as _run

    nc = _bacc.Bacc("TRN2", target_bir_lowering=False, num_devices=1)
    arrays, args = {}, []
    for name in _INS:
        a = _np.ascontiguousarray(inputs[name])
        if name in ('x', 'adj'):
            a = a.reshape(N_TOK, a.shape[-1])
        arrays[f"in_{name}_dram"] = a
        args.append(nc.dram_tensor(f"in_{name}_dram", a.shape, _mybir.dt.from_np(a.dtype), kind="ExternalInput").ap())
    c = _np.zeros((P, C_END), _np.float32)
    c[:, C_ID:C_ID + P] = _np.eye(P)
    c[:, C_TRI:C_TRI + P] = _np.triu(_np.ones((P, P)), 1)
    c[:, C_REV:C_REV + TILES * NE] = _np.tile(NE - _np.arange(NE), TILES)
    c[:, C_TOK:C_TOK + TILES] = _np.arange(TILES) * P + _np.arange(P)[:, None]
    c[:, C_BASE:C_BASE + NE] = _np.arange(NE) * CAP
    c[:, C_G:C_G + NG] = _np.arange(NG)
    arrays["in_consts_dram"] = c
    args.append(nc.dram_tensor("in_consts_dram", c.shape, F32, kind="ExternalInput").ap())
    args.append(nc.dram_tensor("out_0_dram", (N_TOK, D), F32, kind="ExternalOutput").ap())
    gnn_moe_kernel(nc, *args)
    r = _run(nc, [arrays], core_ids=[0])
    return r.results[0]["out_0_dram"].reshape(128, NODES, D)
```

```python
from contextlib import ExitStack

import concourse.bass as bass
from concourse import mybir

ALU = mybir.AluOpType
ACT = mybir.ActivationFunctionType
AX_X = mybir.AxisListType.X
F32 = mybir.dt.float32
F16 = mybir.dt.float16
BF16 = mybir.dt.bfloat16
I32 = mybir.dt.int32
U32 = mybir.dt.uint32

P = 128
D = 128
NODES = 64
N_TOK = 128 * NODES
TILES = 8
BLK = TILES * P
NBLK = N_TOK // BLK
NE = 8
TOP = 2
GRP = 256
GT = GRP // P
NG = N_TOK * TOP // GRP + NE - 1
CAP = N_TOK + GRP
SPARE = NG * GRP - N_TOK * TOP
ROWS = NE * CAP + SPARE
ROW_W = D + 2
NO_TOKEN = 4 * N_TOK
AHEAD = 4
SPAN = 2 * AHEAD
TURNS = (NG - 1) // SPAN
TAIL = NG - SPAN * TURNS
EPS = 1e-5
S_X, S_W, S_H = 1024.0, 64.0, 32.0
HID = [512, 256]
MASKED = [-1.0e9, -9.0e15]
BIG = 3.0e38
C_ID, C_TRI, C_REV, C_TOK, C_BASE, C_G, C_END = 0, 128, 256, 320, 328, 336, 336 + NG


class Chain:

    def __init__(self, eng, sem):
        self.eng, self.sem, self.base, self.k = eng, sem, 0, 0

    def did(self, ins):
        ins.then_inc(self.sem, 1)
        self.k += 1

    def wait(self):
        self.eng.wait_ge(self.sem, self.base + self.k)

    def loop(self, i, first, per):
        self.start = self.base + self.k
        self.base, self.k = self.start + (i - first) * per, 0

    def looped(self, turns, per):
        assert self.k == per, ("signals of a turn", self.k)
        self.base, self.k = self.start + turns * per, 0


def wait_past(eng, sem, value):
    if not (isinstance(value, int) and value <= 0):
        eng.wait_ge(sem, value)


class LayerSems:

    def __init__(self, sem, sems, L):
        self.x_in, self.taken, self.x_done = sems(f"x_in{L}"), sem(f"taken{L}"), sem(f"x_done{L}")
        self.st1, self.st2 = sem(f"st1_{L}"), sem(f"st2_{L}")
        self.xn_ready, self.xT_ps, self.xT_sb = sem(f"xn_ready{L}"), sem(f"xT_ps{L}"), sem(f"xT_sb{L}")
        self.e_ps, self.e_copied, self.e_ready = sem(f"e_ps{L}"), sem(f"e_copied{L}"), sem(f"e_ready{L}")
        self.hs_ps, self.hs_sb = sem(f"hs_ps{L}"), sem(f"hs_sb{L}")
        self.E_sb, self.ET_ps, self.ET_sb = sem(f"E_sb{L}"), sem(f"ET_ps{L}"), sem(f"ET_sb{L}")
        self.att_ps, self.att_sb = sem(f"att_ps{L}"), sem(f"att_sb{L}")
        self.rinv_ready = sem(f"rinv_ready{L}")
        self.xt_ready, self.xtT_ps, self.xtT_sb = sem(f"xt_ready{L}"), sem(f"xtT_ps{L}"), sem(f"xtT_sb{L}")
        self.lg_done, self.lg_copied, self.hot_ready = sem(f"lg_done{L}"), sem(f"lg_copied{L}"), sem(f"hot_ready{L}")
        self.rexp, self.rank_done = sem(f"rexp{L}"), sem(f"rank_done{L}")
        self.ff_ready, self.hi_ready = sem(f"ff_ready{L}"), sem(f"hi_ready{L}")
        self.slots_ready, self.x1w_ready = sem(f"slots_ready{L}"), sem(f"x1w_ready{L}")
        self.scattered, self.stored = sems(f"scattered{L}"), sems(f"stored{L}")
        self.tables, self.pads_out = sem(f"tables{L}"), sem(f"pads_out{L}")
        self.g_loaded, self.y_out = sems(f"g_loaded{L}_", AHEAD), sems(f"y_out{L}_", AHEAD)
        self.gT_ps, self.gT_sb = sem(f"gT_ps{L}"), sem(f"gT_sb{L}")
        self.h_ps, self.act_done, self.h_split = sem(f"h_ps{L}"), sem(f"act_done{L}"), sem(f"h_split{L}")
        self.y_done, self.y_ready, self.placed = sem(f"y_done{L}"), sem(f"y_ready{L}"), sem(f"placed{L}")


def block_at(i, d):
    return 2 * i + d, d % 2, i + d // 2


DVE_SIGNALS = [92, 96]


def gnn_moe_kernel(nc, x, adj, gW0, a_src, a_dst, Wr0, br0, ln_g, ln_b, W1_0, b1_0, W2_0, b2_0,
                   gW1, a_1, Wr1, br1, W1_1, b1_1, W2_1, b2_1, consts, out):
    NC = [h // P for h in HID]

    row_buf = [nc.dram_tensor(f"row_buf{L}", [ROWS, ROW_W], F32, kind="Internal").ap() for L in range(2)]
    x1_buf = [nc.dram_tensor(f"x1_buf{L}", [N_TOK, ROW_W], F32, kind="Internal").ap() for L in range(2)]
    y_buf = [nc.dram_tensor(f"y_buf{L}", [TOP * N_TOK, D], F32, kind="Internal").ap() for L in range(2)]
    Wr, br, b2 = [Wr0, Wr1], [br0, br1], [b2_0, b2_1]
    W1, W2 = [W1_0, W1_1], [W2_0, W2_1]

    with ExitStack() as ctx:
        def sb(name, shape, dt=F32):
            return ctx.enter_context(nc.sbuf_tensor(name, shape, dt))

        def sem(name):
            return ctx.enter_context(nc.semaphore(name))

        def sems(name, n=2):
            return [sem(f"{name}{k}") for k in range(n)]

        cst = sb("cst", [P, C_END])
        ident = cst[:, C_ID:C_ID + P]
        ident16 = sb("ident16", [P, P], F16)
        tri16 = sb("tri16", [P, P], BF16)
        ones16 = sb("ones16", [P, P], BF16)
        vec_rows = sb("vec_rows", [68, P])
        vec_cols = sb("vec_cols", [P, 68])
        V_B1, V_G, V_B, V_A = [0, 32], 48, 56, 64
        att_vec = sb("att_vec", [P, 4, NODES])
        gw = [sb(f"gw{L}", [P, P]) for L in range(2)]
        gwT = [sb(f"gwT{L}", [P, P]) for L in range(2)]
        to_score = sb("to_score", [P, 4, NODES])
        wr = [sb(f"wr{L}", [P, NE]) for L in range(2)]
        br_bc = [sb(f"br_bc{L}", [P, NE]) for L in range(2)]
        b2_bc = [sb(f"b2_bc{L}", [P, NE, D]) for L in range(2)]
        gain = sb("gain", [P, NE])
        b1_cols = [sb("b1_cols0", [P, NE * NC[0]]), sb("b1_cols1", [P, NE * NC[1]])]
        w1 = [sb(f"w1_{L}", [P, NE, 2, HID[L]], F16) for L in range(2)]
        w2 = [sb(f"w2_{L}", [P, NE, NC[L], 2, D], F16) for L in range(2)]
        w_stage = sb("w_stage", [P, NE * 512])

        xin = [sb(f"xin{q}", [P, TILES, ROW_W]) for q in range(2)]
        yin = [sb(f"yin{q}", [P, TOP, TILES, D]) for q in range(2)]
        adj_in = [sb(f"adj_in{q}", [P, TILES, NODES], I32) for q in range(2)]
        stat = sb("stat", [P, 2 * TILES, 6])
        msum, mdif, m2s, mdif2, mean, ve, nt1, nt2, nt3 = (
            sb(n, [P, 2 * TILES]) for n in ("msum", "mdif", "m2s", "mdif2", "mean", "ve", "nt1", "nt2", "nt3"))
        half_bits = sb("half_bits", [P, 2 * TILES], I32)
        rstd1, nmr1 = sb("rstd1", [P, 2 * TILES]), sb("nmr1", [P, 2 * TILES])
        rstd2, nmr2 = sb("rstd2", [P, TILES]), sb("nmr2", [P, TILES])
        xn = sb("xn", [P, TILES, D])
        xnT = sb("xnT", [P, TILES, P])
        xt = sb("xt", [P, TILES, D])
        xtT = sb("xtT", [P, TILES, P])
        keep = sb("keep", [P, TILES * NODES])
        e_sb = sb("e_sb", [P, TILES * NODES])
        e_act = sb("e_act", [P, TILES * NODES])
        e_msk = sb("e_msk", [P, TILES * NODES])
        e_max = sb("e_max", [P, TILES])
        e_dif = sb("e_dif", [P, TILES * NODES])
        pair_e = sb("pair_e", [P, TILES, P])
        pair_eT = sb("pair_eT", [P, TILES, P])
        h_sb = sb("h_sb", [P, TILES, D + 1])
        rinv = sb("rinv", [P, TILES])
        h_new = sb("h_new", [P, TILES, D])
        lg_raw = sb("lg_raw", [P, TILES, NE])
        x1w = [sb(f"x1w{q}", [P, TILES, ROW_W]) for q in range(2)]
        xff = sb("xff", [P, TILES, D])
        pay = [sb(f"pay{q}", [P, TILES, ROW_W]) for q in range(2)]
        slot = [sb(f"slot{q}", [P, TOP, TILES], U32) for q in range(2)]
        tok_run = sb("tok_run", [P, TILES])
        base_run = [sb(f"base_run{L}", [P, NE]) for L in range(2)]
        lg, eq1, ca, lg2, eq2, cb = (sb(n, [P, TILES, NE]) for n in ("lg", "eq1", "ca", "lg2", "eq2", "cb"))
        l_max, r1, l_max2, r2 = (sb(n, [P, TILES]) for n in ("l_max", "r1", "l_max2", "r2"))
        hot = sb("hot", [P, TOP, TILES, NE])
        hot_any = sb("hot_any", [P, TILES, NE], BF16)
        rx = sb("rx", [P, TILES, NE + 1])
        rex = sb("rex", [P, TILES, NE + 1])
        den = sb("den", [P, TILES])
        pos = sb("pos", [P, TILES, NE])
        hot_pos = sb("hot_pos", [P, TOP, TILES, NE])
        slot_f = sb("slot_f", [P, TOP, TILES])
        pad_row = sb("pad_row", [P, ROW_W])
        warm = sb("warm", [P, 2])
        fin_x = [t[:, :, :] for t in (*xin, *x1w, *pay)] + \
                [w_stage[:, k * TILES * ROW_W:(k + 1) * TILES * ROW_W].rearrange("p (t w) -> p t w", w=ROW_W) for k in range(2)]
        fin_y = [[yin[q][:, k, :, :] for k in range(TOP)] for q in range(2)] + \
                [[h_sb[:, :, 0:D], h_new[:, :, :]], [pair_e[:, :, :], pair_eT[:, :, :]]]
        cnt, ng_e, one8, cum = (sb(n, [P, NE]) for n in ("cnt", "ng_e", "one8", "cum"))
        cnt_i, end_i = sb("cnt_i", [P, NE], I32), sb("end_i", [P, NE], I32)
        past = sb("past", [P, NG, NE])
        past_n = sb("past_n", [P, NG, NE])
        grp_e, grp_b, grp_c, grp_r = (sb(n, [P, NG]) for n in ("grp_e", "grp_b", "grp_c", "grp_r"))
        grp_ei, grp_ri = sb("grp_ei", [P, NG], I32), sb("grp_ri", [P, NG], I32)
        g_in = [sb(f"g_in{k}", [P, GT, ROW_W]) for k in range(AHEAD)]
        g_xT = [sb(f"g_xT{q}", [P, 2, GRP], F16) for q in range(2)]
        g_act = [t[:, :, :].rearrange("p t d -> p (t d)").rearrange("p (c r) -> p c r", c=4) for t in (xn, xt)]
        g_h = [t[:, :, :].rearrange("p t d -> p (t d)").bitcast(F16).rearrange("p (h c r) -> p h c r", h=2, c=4)
               for t in (xnT, xtT)] + [sb(f"g_h{k}", [P, 2, 4, GRP], F16)[:, :, :, :] for k in (2, 3)]
        g_y = [sb(f"g_y{k}", [P, GT, D]) for k in range(AHEAD)]
        g_k = sb("g_k", [P, GT])
        g_row = [sb(f"g_row{k}", [P, GT]) for k in range(AHEAD)]
        g_dst = [sb(f"g_dst{k}", [P, GT], U32) for k in range(AHEAD)]

        bank = [ctx.enter_context(nc.psum_tensor(f"bank{k}", [P, 512], F32)) for k in range(8)]
        lg_ps = bank[7][:, 0:TILES * NE]
        rank_ps = bank[7][:, 64:64 + TILES * NE]
        tot_ps = bank[7][:, 128:128 + NE]
        att_parts = [(bank[b][:, at:at + m * (D + 1)].rearrange("p (t d) -> p t d", d=D + 1), t, m)
                     for b, at, t, m in ((5, 0, 0, 3), (6, 0, 3, 3), (7, 128 + NE, 6, 2))]
        att_tile = [att[:, k, :] for att, t, m in att_parts for k in range(m)]

        cst_in, vec_in, gw_in, rt_in = sem("cst_in"), sem("vec_in"), sem("gw_in"), sem("rt_in")
        stage_in, stage_used = sem("stage_in"), sem("stage_used")
        set_ready, vecT_ps, vec_ready, set_ps, set_sb, ttl_ps = (
            sem("set_ready"), sem("vecT_ps"), sem("vec_ready"), sem("set_ps"), sem("set_sb"), sem("ttl_ps"))
        dve_chain = sem("dve_chain")
        bw_ps, pool_turns = sem("bw_ps"), sem("pool_turns")
        spare_out = sem("spare_out")
        w_ready = sems("w_ready")
        fin_in, fin_done, out_st = sems("fin_in", NBLK), sem("fin_done"), sems("out_st", NBLK)

        SL = []
        for L in range(2):
            s = LayerSems(sem, sems, L)
            SL.append(s)

        block = ctx.enter_context(nc.Block())

        def table_values(eng, table, g, n, top):
            at = table[0:1, g:g + n] if isinstance(g, int) else table[0:1, bass.ds(g, n)]
            return nc.values_load_multi_w_load_instructions(at, engines=[eng], min_val=0, max_val=top,
                skip_runtime_bounds_check_because="the table's values are clamped to this range when it is made")[1]
        per = 2
        hid_v = [W1[L].rearrange("e d h -> d e h") for L in range(2)]
        out_v = [W2[L].rearrange("e (c p) d -> p (e c) d", p=P) for L in range(2)]

        @block.sync
        def _(sp):
            tok3 = lambda ap, n: ap[bass.ds(n * BLK, BLK), :].rearrange("(t p) w -> p t w", p=P)

            def load_early(L, n, q):
                sp.dma_start(adj_in[q][:, :, :], tok3(adj, n)).then_inc(SL[L].x_in[q], 16)
                load_results(L, n, q)

            def load_results(L, n, q):
                s = SL[L]
                if L == 1:
                    for k in range(TOP):
                        sp.dma_start(yin[q][:, k, :, :], y_buf[0][bass.ds(n * BLK + k * N_TOK, BLK), :].rearrange(
                            "(t p) w -> p t w", p=P)).then_inc(s.x_in[q], 16)

            def load_x(L, n, q):
                if L == 0:
                    sp.dma_start(xin[q][:, :, 0:D], tok3(x, n)).then_inc(SL[L].x_in[q], 16)
                else:
                    sp.dma_start(xin[q][:, :, :], tok3(x1_buf[0], n)).then_inc(SL[L].x_in[q], 16)

            def store(L, n, q):
                sp.wait_ge(SL[L].x1w_ready, n + 1)
                sp.dma_start(tok3(x1_buf[L], n), x1w[q][:, :, :]).then_inc(SL[L].stored[q], 16)

            stages = [(out_v[0], NE * HID[0]), (hid_v[0], NE * HID[0]), (out_v[1], NE * HID[1]), (hid_v[1], NE * HID[1])]

            def load_stage(m):
                if m:
                    sp.wait_ge(stage_used, m)
                src, width = stages[m]
                sp.dma_start(w_stage[:, 0:width].rearrange("p (a b) -> p a b", a=src.shape[1]), src).then_inc(stage_in, 16)

            def setup():
                load_x(0, 0, 0)
                load_early(0, 0, 0)
                sp.dma_start(cst[:, :], consts).then_inc(cst_in, 16)
                rows = [(b1_0.rearrange("e (c p) -> (e c) p", p=P), V_B1[0]), (b1_1.rearrange("e (c p) -> (e c) p", p=P), V_B1[1]),
                        (ln_g, V_G), (ln_b, V_B), (a_src.unsqueeze(0), V_A), (a_dst.unsqueeze(0), V_A + 1),
                        (a_1.rearrange("(k p) o -> k (p o)", p=P), V_A + 2)]
                for src, at in rows:
                    sp.dma_start(vec_rows[at:at + src.shape[0], :], src).then_inc(vec_in, 16)
                sp.dma_start(gw[0][:, :], gW0).then_inc(gw_in, 16)
                sp.dma_start(gw[1][:, :], gW1).then_inc(gw_in, 16)
                load_stage(0)
                load_x(0, 1, 1)
                load_early(0, 1, 1)
                for L in range(2):
                    sp.dma_start(wr[L][:, :], Wr[L]).then_inc(rt_in, 16)
                    sp.dma_start(br_bc[L][:, :], br[L].unsqueeze(0).to_broadcast([P, NE])).then_inc(rt_in, 16)
                    sp.dma_start(b2_bc[L][:, :, :], b2[L].unsqueeze(0).to_broadcast([P, NE, D])).then_inc(rt_in, 16)

            def blocks(L):
                s = SL[L]
                if L == 1:
                    for n in range(2):
                        load_results(L, n, n)

                def step(i, d):
                    n, q, turn = block_at(i, d)
                    if isinstance(n, int) and n < 0 or not isinstance(n, int) or n + 3 < NBLK:
                        sp.wait_ge(s.taken, n + 2)
                        load_early(L, n + 3, (q + 1) % 2)
                    if not isinstance(n, int) or 0 <= n < NBLK - 2:
                        sp.wait_ge(s.x_done, n + 1)
                        load_x(L, n + 2, q)
                    if not isinstance(n, int) or n >= 1:
                        store(L, n - 1, (q + 1) % 2)
                step(0, -1)
                step(0, 0)
                load_stage(2 * L + 1)
                if L == 0:
                    sp.wait_ge(set_ready, 1)
                    for LL in range(2):
                        sp.dma_start(row_buf[LL][NE * CAP:ROWS, :].rearrange("(t p) w -> p t w", p=P),
                                     pad_row[:, :].unsqueeze(1).to_broadcast([P, SPARE // P, ROW_W])).then_inc(spare_out, 16)
                with sp.Fori(0, (NBLK - 4) // 2) as i:
                    for d in (1, 2):
                        step(i, d)
                for n in range(NBLK - 3, NBLK + 1):
                    step(0, n)

            def groups(L):
                s = SL[L]
                sp.wait_ge(s.tables, 1)
                for e in range(NE):
                    end = sp.value_load(end_i[0:1, e:e + 1], min_val=0, max_val=NE * CAP - GRP)
                    sp.dma_start(row_buf[L][bass.ds(end, GRP), :].rearrange("(t p) w -> p t w", p=P),
                                 pad_row[:, :].unsqueeze(1).to_broadcast([P, GT, ROW_W])).then_inc(s.pads_out, 16)
                for q in range(2):
                    sp.wait_ge(s.scattered[q], 16 * TOP * TILES * NBLK // 2)
                sp.wait_ge(s.pads_out, 16 * NE)
                if L == 0:
                    sp.wait_ge(spare_out, 32)

                def load_group(g, k):
                    r = sp.value_load(grp_ri[0:1, bass.ds(g, 1)], min_val=0, max_val=ROWS - GRP)
                    sp.dma_start(g_in[k][:, :, :], row_buf[L][bass.ds(r, GRP), :].rearrange("(t p) w -> p t w", p=P)
                                 ).then_inc(s.g_loaded[k], 16)
                for k in range(AHEAD):
                    load_group(k, k)

                def load_next(g, k):
                    sp.wait_ge(s.gT_ps, g + 1)
                    sp.wait_ge(s.placed, g + 1)
                    load_group(g + AHEAD, k)
                with sp.Fori(0, NG // AHEAD - 1) as i:
                    for k in range(AHEAD):
                        load_next(AHEAD * i + k, k)
                for g in range(NG // AHEAD * AHEAD - AHEAD, NG - AHEAD):
                    load_next(g, g % AHEAD)

            def all_written(L):
                for k in range(AHEAD):
                    sp.wait_ge(SL[L].y_out[k], 16 * GT * len(range(k, NG, AHEAD)))

            def all_stored(L):
                for q in range(2):
                    sp.wait_ge(SL[L].stored[q], 16 * NBLK // 2)

            setup()
            blocks(0)
            groups(0)
            load_stage(2)
            all_stored(0)
            for n in range(2):
                load_x(1, n, n)
                sp.dma_start(adj_in[n][:, :, :], tok3(adj, n)).then_inc(SL[1].x_in[n], 16)
            all_written(0)
            blocks(1)
            groups(1)
            all_stored(1)

            def last_x(n):
                sp.dma_start(fin_x[n], tok3(x1_buf[1], n)).then_inc(fin_in[n], 16)

            def last_results(n):
                for k in range(TOP):
                    sp.dma_start(fin_y[n % len(fin_y)][k], y_buf[1][n * BLK + k * N_TOK:(n + 1) * BLK + k * N_TOK, :].rearrange(
                        "(t p) w -> p t w", p=P)).then_inc(fin_in[n], 16)
            sp.wait_ge(stage_used, 4)
            for n in range(NBLK):
                last_x(n)
            all_written(1)
            for n in range(len(fin_y)):
                last_results(n)
            for n in range(NBLK):
                sp.wait_ge(fin_done, n + 1)
                sp.dma_start(tok3(out, n), fin_x[n][:, :, 0:D]).then_inc(out_st[n], 16)
                if n + len(fin_y) < NBLK:
                    last_results(n + len(fin_y))
            for n in range(NBLK):
                sp.wait_ge(out_st[n], 16)

        @block.gpsimd
        def _(pool):
            for L in range(2):
                s = SL[L]
                with pool.Fori(0, NBLK // per) as i:
                    for q in range(2):
                        pool.wait_ge(s.slots_ready, per * i + q + 1)
                        pool.sem_inc(pool_turns, 1)
                        for k in range(TOP):
                            for t in range(TILES):
                                pool.indirect_dma_start(
                                    row_buf[L][:, :], bass.IndirectOffsetOnAxis(ap=slot[q][:, k, t:t + 1], axis=0),
                                    pay[q][:, t, :], None).then_inc(s.scattered[q], 16)

                def scatter_results(g, k):
                    pool.wait_ge(s.y_ready, g + 1)
                    pool.sem_inc(pool_turns, 1)
                    for t in range(GT):
                        pool.indirect_dma_start(
                            y_buf[L][:, :], bass.IndirectOffsetOnAxis(ap=g_dst[k][:, t:t + 1], axis=0),
                            g_y[k][:, t, :], None, bounds_check=TOP * N_TOK - 1, oob_is_err=False
                        ).then_inc(s.y_out[k], 16)
                with pool.Fori(0, NG // AHEAD) as i:
                    for k in range(AHEAD):
                        scatter_results(AHEAD * i + k, k)
                for g in range(NG // AHEAD * AHEAD, NG):
                    scatter_results(g, g % AHEAD)

        @block.tensor
        def _(pe):
            pe.wait_ge(vec_in, 16 * 7)
            pe.wait_ge(cst_in, 16)
            nc.tensor.transpose(bank[0][:, 0:68], vec_rows[:, :], ident[0:68, 0:68]).then_inc(vecT_ps, 1)
            pe.wait_ge(gw_in, 32)
            for L in range(2):
                last = nc.tensor.transpose(bank[1][:, L * P:(L + 1) * P], gw[L][:, :], ident)
            last.then_inc(set_ps, 1)
            pe.wait_ge(vec_ready, 1)
            for k in range(4):
                lhsT = gw[0] if k < 2 else gwT[1]
                last = nc.tensor.matmul(bank[2][:, k * NODES:(k + 1) * NODES], lhsT[:, :], att_vec[:, k, :],
                                        start=True, stop=True)
            last.then_inc(ttl_ps, 1)
            pe.wait_ge(set_sb, 1)

            def transpose_tiles(src, done, ready=None, n=0):
                for t in range(TILES):
                    if ready is not None and t % 4 == 0:
                        pe.wait_ge(ready, 2 * n + 1 + t // 4)
                    last = nc.tensor.transpose(bank[t // 4][:, (t % 4) * P:(t % 4 + 1) * P], src[:, t, :], ident)
                    if t % 4 == 3:
                        last.then_inc(done, 1)

            def transpose_input(L, n):
                transpose_tiles(xn, SL[L].xT_ps, SL[L].xn_ready, n)

            def features(L, n):
                s = SL[L]
                w_h = gwT[0] if L == 0 else gw[1]
                halves = xnT[:, :, :].rearrange("p t (g j) -> p t g j", g=2)
                for k in range(2):
                    pe.wait_ge(s.xT_sb, 2 * n + 1 + k)
                    cols = slice(4 * k * NODES, 4 * (k + 1) * NODES)
                    for g in range(2):
                        nc.tensor.matmul(bank[2][g * NODES:(g + 1) * NODES, cols], to_score[:, 2 * L + 1, :],
                                         halves[:, 4 * k:4 * k + 4, g, :], start=True, stop=False, skip_group_check=True)
                    for t in range(4 * k, 4 * k + 4):
                        last = nc.tensor.matmul(bank[2][:, t * NODES:(t + 1) * NODES], xnT[:, t, :], to_score[:, 2 * L, :],
                                                start=False, stop=(t % 4 == 3), skip_group_check=True)
                last.then_inc(s.e_ps, 1)
                for t in range(TILES):
                    last = nc.tensor.matmul(bank[3 + t // 4][:, (t % 4) * P:(t % 4 + 1) * P], xnT[:, t, :], w_h[:, :],
                                            start=True, stop=True)
                last.then_inc(s.hs_ps, 1)

            def transpose_exps(L, n):
                pe.wait_ge(SL[L].E_sb, n + 1)
                transpose_tiles(pair_e, SL[L].ET_ps)

            def attention(L, n):
                s = SL[L]
                pe.wait_ge(s.hs_sb, n + 1)
                for t in range(TILES):
                    if t % 4 == 0:
                        pe.wait_ge(s.ET_sb, 2 * n + 1 + t // 4)
                    last = nc.tensor.matmul(att_tile[t], pair_eT[:, t, :], h_sb[:, t, :],
                                            start=True, stop=True)
                last.then_inc(s.att_ps, 1)

            def ranks(L, n):
                s = SL[L]
                pe.wait_ge(s.hot_ready, n + 1)
                hot_v = hot_any[:, :, :].rearrange("p t e -> p (t e)")
                nc.tensor.matmul(rank_ps, tri16[:, :], hot_v, start=True, stop=False, skip_group_check=True)
                for d in range(1, TILES):
                    nc.tensor.matmul(rank_ps[:, d * NE:], ones16[:, :], hot_v[:, 0:(TILES - d) * NE],
                                     start=False, stop=(d == TILES - 1), skip_group_check=True)
                for t in range(TILES):
                    last = nc.tensor.matmul(tot_ps, ones16[:, :], hot_v[:, t * NE:(t + 1) * NE],
                                            start=(t == 0), stop=(t == TILES - 1), skip_group_check=True)
                last.then_inc(s.rank_done, 1)

            def transpose_x1(L, n):
                transpose_tiles(xt, SL[L].xtT_ps, SL[L].xt_ready, n)

            def logits(L, n):
                s = SL[L]
                for t in range(TILES):
                    if t % 4 == 0:
                        pe.wait_ge(s.xtT_sb, 2 * n + 1 + t // 4)
                    last = nc.tensor.matmul(lg_ps[:, t * NE:(t + 1) * NE], xtT[:, t, :], wr[L][:, :], start=True, stop=True)
                last.then_inc(s.lg_done, 1)

            def blocks(L):
                def step(n, first=False, last=False):
                    if not first:
                        logits(L, n - 1)
                    transpose_exps(L, n)
                    attention(L, n)
                    if not first:
                        pe.wait_ge(SL[L].x_done if L == 0 else SL[L].rinv_ready, n + 1)
                        ranks(L, n - 1)
                    if not last:
                        transpose_input(L, n + 1)
                        features(L, n + 1)
                    transpose_x1(L, n)
                transpose_input(L, 0)
                features(L, 0)
                step(0, first=True)
                pe.wait_ge(rt_in, 16 * 6)
                with pe.Fori(0, NBLK // per - 1) as i:
                    for d in (1, 2):
                        step(per * i + d)
                step(NBLK - 1, last=True)
                logits(L, NBLK - 1)
                ranks(L, NBLK - 1)

            def groups(L):
                s = SL[L]
                x_ps = [bank[b][:, 0:GRP].bitcast(F16).rearrange("p (h n) -> p h n", h=2) for b in (4, 7)]

                def to_feature_rows(k, turn):
                    q, turn = k % 2, SPAN // AHEAD * turn + k // AHEAD
                    pe.wait_ge(s.g_loaded[k % AHEAD], 16 * (turn + 1))
                    rows16 = g_in[k % AHEAD][:, :, :].bitcast(F16)
                    for hl in range(2):
                        for t in range(GT):
                            last = nc.tensor.transpose(x_ps[q][:, hl, t * P:(t + 1) * P],
                                                       rows16[:, t, hl * D:(hl + 1) * D], ident16[:, :])
                    last.then_inc(s.gT_ps, 1)

                def experts(g, n):
                    return table_values(mybir.EngineType.PE, grp_ei, g, n, NE - 1)

                def up(g, q, e):
                    wait_past(pe, s.act_done, (g - 1) * NC[L])
                    pe.wait_ge(s.gT_sb, g + 1)
                    w = w1[L][:, :, :, :].rearrange("p e a h -> p (e a h)")
                    for c in range(NC[L]):
                        dst = bank[2 * q + c // 2][:, (c % 2) * GRP:(c % 2 + 1) * GRP]
                        for m, (wp, xp) in enumerate(((0, 0), (0, 1), (1, 0))):
                            last = nc.tensor.matmul(dst, w[:, bass.ds(e * (2 * HID[L]) + (wp * HID[L] + c * P), P)],
                                                    g_xT[q][:, xp, :], start=(m == 0), stop=(m == 2))
                        if c % 2:
                            last.then_inc(s.h_ps, 1)

                def down(g, k, e):
                    w = w2[L][:, :, :, :, :].rearrange("p e c a d -> p (e c a d)")
                    wait_past(pe, s.y_ready, g - 1)
                    hid = g_h[k % AHEAD]
                    pe.wait_ge(s.h_split, (NC[L] // 2) * (g + 1))
                    for t in range(GT):
                        m = 0
                        for c in range(NC[L]):
                            for wp, hp in ((0, 0), (0, 1), (1, 0)):
                                last = nc.tensor.matmul(
                                    bank[5 + k % 2][:, t * D:(t + 1) * D], hid[:, hp, c, t * P:(t + 1) * P],
                                    w[:, bass.ds(e * (2 * HID[L]) + (2 * c + wp) * D, D)],
                                    start=(m == 0), stop=(m == 3 * NC[L] - 1))
                                m += 1
                    last.then_inc(s.y_done, 1)

                pe.wait_ge(s.tables, 1)
                pe.wait_ge(w_ready[L], 1)
                for k in range(2):
                    to_feature_rows(k, 0)
                es = experts(0, 2)
                up(0, 0, es[0])
                to_feature_rows(2, 0)
                up(1, 1, es[1])

                def turn(i, last=False):
                    n = TAIL if last else SPAN
                    es = experts(SPAN * i, n if last else n + 2)
                    for k in range(n):
                        g = SPAN * i + k
                        if not last or k + 3 < n:
                            to_feature_rows(k + 3, i)
                        if not last or k + 2 < n:
                            up(g + 2, k % 2, es[k + 2])
                        down(g, k, es[k])
                turn(0)
                with pe.Fori(1, TURNS) as i:
                    turn(i)
                turn(TURNS, last=True)

            for L in range(2):
                blocks(L)
                if L == 0:
                    pe.wait_ge(stage_in, 32)
                    for e in range(NE):
                        for c in range(NC[0]):
                            k = e * NC[0] + c
                            last = nc.tensor.matmul(bank[0][:, k:k + 1], w_stage[:, e * HID[0] + c * P:e * HID[0] + (c + 1) * P],
                                                    vec_cols[:, V_B + e:V_B + e + 1], start=True, stop=True)
                    last.then_inc(bw_ps, 1)
                groups(L)

        @block.scalar
        def _(act):
            act.wait_ge(set_sb, 1)

            def copy_bank(b, dst, k, func=ACT.Copy):
                return nc.scalar.activation(dst[:, 4 * k:4 * k + 4, 0:D], bank[b + k][:, :].rearrange("p (t d) -> p t d", d=P), func)

            def copy_transposed(n, ps, dst, copied):
                for k in range(2):
                    act.wait_ge(ps, 2 * n + 1 + k)
                    copy_bank(0, dst, k).then_inc(copied, 1)

            def normalise(dst, src, rstd, nmr, at, done):
                for t in range(TILES):
                    last = nc.scalar.activation(dst[:, t, :], src[:, t, :], ACT.Identity, bias=nmr[:, at + t:at + t + 1],
                                                scale=rstd[:, at + t:at + t + 1])
                    if t % 4 == 3:
                        last.then_inc(done, 1)

            def load_table(func):
                nc.scalar.activation(warm[:, 1:2], warm[:, 0:1], func)

            def norm_input(L, n, q):
                act.wait_ge(SL[L].st1, n + 1)
                normalise(xn, xin[q][:, :, 0:D], rstd1, nmr1, 0, SL[L].xn_ready)

            def copy_logits(L, n):
                act.wait_ge(SL[L].lg_done, n + 1)
                nc.scalar.activation(lg_raw[:, :, :], lg_ps.rearrange("p (t e) -> p t e", e=NE), ACT.Copy).then_inc(SL[L].lg_copied, 1)

            def attention(L, n, first):
                s = SL[L]
                act.wait_ge(s.e_ready, n + 1)
                for g in range(2):
                    r = slice(g * NODES, (g + 1) * NODES)
                    last = nc.scalar.activation(pair_e[r, :, r], e_dif[r, :].rearrange("p (t j) -> p t j", j=NODES), ACT.Exp)
                last.then_inc(s.E_sb, 1)
                if not first:
                    copy_logits(L, n - 1)
                copy_transposed(n, s.ET_ps, pair_eT, s.ET_sb)

            def input_columns(L, n):
                copy_transposed(n, SL[L].xT_ps, xnT, SL[L].xT_sb)

            def copy_scores(L, n):
                s = SL[L]
                act.wait_ge(s.e_ps, n + 1)
                nc.scalar.activation(e_sb[:, :], bank[2][:, :], ACT.Copy).then_inc(s.e_copied, 1)

            def copy_features(L, n):
                s = SL[L]
                act.wait_ge(s.hs_ps, n + 1)
                copy_bank(3, h_sb, 0)
                copy_bank(3, h_sb, 1).then_inc(s.hs_sb, 1)

            def expert_norm(L, n):
                act.wait_ge(SL[L].st1, n + 3)
                normalise(xff, xt, rstd1, nmr1, TILES, SL[L].ff_ready)

            def high_parts(L, n, q, turn):
                s = SL[L]
                if L == 0:
                    act.wait_ge(s.ff_ready, 2 * n + 2)
                wait_past(act, s.scattered[q], 16 * TOP * TILES * turn)
                nc.scalar.activation(pay[q][:, :, :].bitcast(F16)[:, :, 0:D], (xff if L == 0 else xt)[:, :, :],
                                     ACT.Copy, scale=S_X).then_inc(s.hi_ready, 1)

            def router(L, n):
                act.wait_ge(SL[L].hot_ready, n + 1)
                nc.scalar.activation(rex[:, :, :], rx[:, :, :], ACT.Exp).then_inc(SL[L].rexp, 1)

            def blocks(L):
                s = SL[L]

                def step(i, d, first=False, last=False):
                    n, q, turn = block_at(i, d)
                    attention(L, n, first)
                    if L == 1 and not first:
                        high_parts(L, *block_at(i, d - 1))
                    if L == 1:
                        act.wait_ge(s.att_ps, n + 1)
                        for att, t, m in att_parts:
                            last_copy = nc.scalar.activation(h_new[:, t:t + m, :], att[:, :, 0:D], ACT.Relu)
                        last_copy.then_inc(s.att_sb, 1)
                    if not first:
                        router(L, n - 1)
                    if not last:
                        norm_input(L, n + 1, (q + 1) % 2)
                    if not last:
                        input_columns(L, n + 1)
                    if not first:
                        if L == 0:
                            expert_norm(L, n - 1)
                            high_parts(L, *block_at(i, d - 1))
                    if not last:
                        copy_scores(L, n + 1)
                    act.wait_ge(s.st2, n + 1)
                    wait_past(act, s.hi_ready, n)
                    normalise(xt, x1w[q][:, :, 0:D], rstd2, nmr2, 0, s.xt_ready)
                    if not last:
                        copy_features(L, n + 1)
                    copy_transposed(n, s.xtT_ps, xtT, s.xtT_sb)
                load_table(ACT.Exp)
                norm_input(L, 0, 0)
                input_columns(L, 0)
                copy_scores(L, 0)
                copy_features(L, 0)
                step(0, 0, first=True)
                with act.Fori(0, NBLK // per - 1) as i:
                    for d in (1, 2):
                        step(i, d)
                step(0, NBLK - 1, last=True)
                copy_logits(L, NBLK - 1)
                router(L, NBLK - 1)
                if L == 0:
                    expert_norm(L, NBLK - 1)
                high_parts(L, *block_at(0, NBLK - 1))

            def groups(L):
                s = SL[L]
                x_ps = [bank[b][:, 0:GRP].bitcast(F16).rearrange("p (h n) -> p h n", h=2) for b in (4, 7)]

                def copy_x(g, q):
                    act.wait_ge(s.gT_ps, g + 1)
                    nc.scalar.activation(g_xT[q][:, :, :], x_ps[q], ACT.Copy).then_inc(s.gT_sb, 1)

                def gelu(g, q, e):
                    wait_past(act, s.h_split, (g - 1) * (NC[L] // 2))
                    for c in range(NC[L]):
                        if c % 2 == 0:
                            act.wait_ge(s.h_ps, NC[L] // 2 * g + c // 2 + 1)
                        nc.scalar.activation(g_act[q][:, c, :], bank[2 * q + c // 2][:, (c % 2) * GRP:(c % 2 + 1) * GRP],
                                             ACT.Gelu, bias=b1_cols[L][:, bass.ds(e * NC[L] + c, 1)],
                                             scale=1.0 / (S_X * S_W)).then_inc(s.act_done, 1)

                def experts(g, n):
                    return table_values(mybir.EngineType.Activation, grp_ei, g, n, NE - 1)
                load_table(ACT.Gelu)
                act.wait_ge(s.tables, 1)
                act.wait_ge(w_ready[L], 1)
                for k in range(2):
                    copy_x(k, k)
                es = experts(0, 2)
                gelu(0, 0, es[0])
                copy_x(2, 0)
                gelu(1, 1, es[1])

                def turn(i, last=False):
                    n = TAIL - 2 if last else SPAN
                    es = experts(SPAN * i + 2, n)
                    for k in range(n):
                        if not last or k < n - 1:
                            copy_x(SPAN * i + k + 3, (k + 1) % 2)
                        gelu(SPAN * i + k + 2, k % 2, es[k])
                with act.Fori(0, TURNS) as i:
                    turn(i)
                turn(TURNS, last=True)

            for L in range(2):
                blocks(L)
                groups(L)

        @block.vector
        def _(dve):
            ch = Chain(dve, dve_chain)
            V = nc.vector
            V.memset(ones16[:, :], 1.0)
            V.memset(one8[:, :], 1.0)
            V.memset(pair_e[:, :, :], 0.0)
            V.memset(warm[:, :], 0.0)
            V.memset(h_sb[:, :, D:D + 1], 1.0)
            ch.did(V.memset(pad_row[:, :], 0.0))
            ch.wait()
            V.memset(pad_row[:, D:D + 1], float(NO_TOKEN)).then_inc(set_ready, 1)
            dve.wait_ge(cst_in, 16)
            V.tensor_copy(ident16[:, :], ident)
            V.tensor_copy(tri16[:, :], cst[:, C_TRI:C_TRI + P])
            V.tensor_copy(tok_run[:, :], cst[:, C_TOK:C_TOK + TILES])
            for L in range(2):
                V.tensor_copy(base_run[L][:, :], cst[:, C_BASE:C_BASE + NE])
            dve.wait_ge(vecT_ps, 1)
            ch.did(V.tensor_copy(vec_cols[:, :], bank[0][:, 0:68]))
            ch.wait()
            V.tensor_scalar(gain[:, :], vec_cols[:, V_G:V_G + NE], S_W, None, ALU.mult)
            V.tensor_copy(b1_cols[1][:, :], vec_cols[:, V_B1[1]:V_B1[1] + NE * NC[1]])
            V.tensor_copy(att_vec[:, :, :], vec_cols[:, V_A:V_A + 4].unsqueeze(2).to_broadcast([P, 4, NODES]))
            dve.wait_ge(set_ps, 1)
            V.tensor_copy(gwT[0][:, :], bank[1][:, 0:P])
            V.tensor_copy(gwT[1][:, :], bank[1][:, P:2 * P]).then_inc(vec_ready, 1)
            dve.wait_ge(ttl_ps, 1)
            V.tensor_copy(to_score[:, :, :], bank[2][:, 0:4 * NODES].rearrange("p (k j) -> p k j", j=NODES)).then_inc(set_sb, 1)
            dve.wait_ge(set_sb, 1)

            rev = cst[:, C_REV:C_REV + TILES * NE].rearrange("p (t e) -> p t e", e=NE)
            bc = lambda ap: ap.unsqueeze(2).to_broadcast([P, TILES, NE])

            def statistics(srcs, rstd, nmr, beside):
                def pause():
                    next(beside, None)
                    ch.wait()
                W = TILES * len(srcs)
                for m, src in enumerate(srcs):
                    for t in range(TILES):
                        last = V.bn_stats(stat[:, m * TILES + t, :], src[:, t, :])
                ch.did(last)
                pause()
                w = slice(0, W)
                V.tensor_tensor(msum[:, w], stat[:, w, 1], stat[:, w, 4], ALU.add)
                V.scalar_tensor_tensor(m2s[:, w], stat[:, w, 2], EPS * D, stat[:, w, 5], ALU.add, ALU.add)
                ch.did(V.tensor_tensor(mdif[:, w], stat[:, w, 1], stat[:, w, 4], ALU.subtract))
                pause()
                V.tensor_scalar(mean[:, w], msum[:, w], -0.5, None, ALU.mult)
                ch.did(V.tensor_tensor(mdif2[:, w], mdif[:, w], mdif[:, w], ALU.mult))
                pause()
                ch.did(V.scalar_tensor_tensor(ve[:, w], mdif2[:, w], D / 4.0, m2s[:, w], ALU.mult, ALU.add))
                pause()
                ch.did(V.tensor_scalar(half_bits[:, w], ve[:, w].bitcast(I32), 1, None, ALU.logical_shift_right))
                pause()
                ch.did(V.tensor_scalar(nt1[:, w].bitcast(I32), half_bits[:, w], -1.0, float(0x5f3759df), ALU.mult, ALU.add))
                pause()
                ch.did(V.tensor_tensor(nt2[:, w], nt1[:, w], nt1[:, w], ALU.mult))
                pause()
                ch.did(V.tensor_tensor(nt2[:, w], nt2[:, w], ve[:, w], ALU.mult))
                pause()
                ch.did(V.scalar_tensor_tensor(nt3[:, w], nt2[:, w], -10.0 / 3.0, nt2[:, w], ALU.add, ALU.mult))
                pause()
                ch.did(V.scalar_tensor_tensor(nt1[:, w], nt3[:, w], 5.0, nt1[:, w], ALU.add, ALU.mult))
                pause()
                ch.did(V.tensor_tensor(nt2[:, w], nt1[:, w], nt1[:, w], ALU.mult))
                pause()
                ch.did(V.scalar_tensor_tensor(nt2[:, w], nt2[:, w], -0.5 * 0.375 ** 3 * D ** 0.5, ve[:, w], ALU.mult, ALU.mult))
                pause()
                ch.did(V.scalar_tensor_tensor(rstd[:, w], nt2[:, w], 1.5 * 0.375 * D ** 0.5, nt1[:, w], ALU.add, ALU.mult))
                pause()
                return V.tensor_tensor(nmr[:, w], mean[:, w], rstd[:, w], ALU.mult)

            def finish_steps(beside):
                for _ in beside:
                    ch.wait()

            def add_experts(src, y, part=range(TOP)):
                for k in part:
                    for t in range(TILES):
                        last = V.scalar_tensor_tensor(src[:, t, 0:D], y[k][:, t, :], src[:, t, D + k:D + k + 1],
                                                      src[:, t, 0:D], ALU.mult, ALU.add)
                    if k == 0:
                        ch.did(last)
                        if len(part) == 2:
                            ch.wait()
                return last

            def scores(L, n):
                s = SL[L]
                dve.wait_ge(s.e_copied, n + 1)
                ch.did(V.scalar_tensor_tensor(e_act[:, :], e_sb[:, :], 0.2, e_sb[:, :], ALU.mult, ALU.max))
                ch.wait()
                ch.did(V.scalar_tensor_tensor(e_msk[:, :], keep[:, :], MASKED[L], e_act[:, :], ALU.add, ALU.min))
                ch.wait()
                e3 = e_msk[:, :].rearrange("p (t j) -> p t j", j=NODES)
                ch.did(V.tensor_reduce(e_max[:, :], e3, AX_X, ALU.max))
                ch.wait()
                V.tensor_tensor(e_dif[:, :].rearrange("p (t j) -> p t j", j=NODES), e3,
                                e_max[:, :].unsqueeze(2).to_broadcast([P, TILES, NODES]), ALU.subtract).then_inc(s.e_ready, 1)

            def arrive(L, n, q, turn):
                dve.wait_ge(SL[L].x_in[q], (32 if L == 0 else 64) * (turn + 1))
                if L == 1:
                    add_experts(xin[q], [yin[q][:, k, :, :] for k in range(TOP)], (0,))

            def take_in(L, n, q, turn):
                s = SL[L]
                if L == 1:
                    ch.wait()
                    ch.did(add_experts(xin[q], [yin[q][:, k, :, :] for k in range(TOP)], (1,)))
                    ch.wait()
                V.tensor_scalar(keep[:, :], adj_in[q][:, :, :].rearrange("p t j -> p (t j)"), 0.0, BIG,
                                ALU.not_equal if L == 0 else ALU.is_gt, ALU.mult).then_inc(s.taken, 1)

            def add_attention(L, n, q, turn, beside):
                s = SL[L]
                dve.wait_ge(s.att_ps if L == 0 else s.att_sb, n + 1)
                for att, t, m in att_parts:
                    last = V.reciprocal(rinv[:, t:t + m], att[:, :, D])
                last.then_inc(s.rinv_ready, 1)
                wait_past(dve, s.stored[q], 16 * turn)
                dve.wait_ge(s.rinv_ready, n + 1)
                for t in range(TILES):
                    att = att_tile[t][:, 0:D] if L == 0 else h_new[:, t, :]
                    last = V.scalar_tensor_tensor(x1w[q][:, t, 0:D], att, rinv[:, t:t + 1], xin[q][:, t, 0:D], ALU.mult, ALU.add)
                last.then_inc(s.x_done, 1)
                dve.wait_ge(s.x_done, n + 1)
                statistics([x1w[q][:, :, 0:D]], rstd2, nmr2, beside).then_inc(s.st2, 1)

            def route(L, n, q, turn):
                s = SL[L]
                for _ in range(3):
                    yield
                dve.wait_ge(s.lg_copied, n + 1)
                wait_past(dve, s.scattered[q], 16 * TOP * TILES * turn)
                V.tensor_copy(pay[q][:, :, D], tok_run[:, :])
                ch.did(V.tensor_tensor(lg[:, :, :], lg_raw[:, :, :],
                                       br_bc[L][:, :].unsqueeze(1).to_broadcast([P, TILES, NE]), ALU.add))
                yield
                for k, (val, vmax, eq, cand, cmax) in enumerate(((lg, l_max, eq1, ca, r1), (lg2, l_max2, eq2, cb, r2))):
                    ch.did(V.tensor_reduce(vmax[:, :], val[:, :, :], AX_X, ALU.max))
                    yield
                    ch.did(V.tensor_tensor(eq[:, :, :], val[:, :, :], bc(vmax[:, :]), ALU.is_equal))
                    yield
                    ch.did(V.tensor_tensor(cand[:, :, :], eq[:, :, :], rev, ALU.mult))
                    yield
                    ch.did(V.tensor_reduce(cmax[:, :], cand[:, :, :], AX_X, ALU.max))
                    yield
                    ch.did(V.tensor_tensor(hot[:, k, :, :], cand[:, :, :], bc(cmax[:, :]), ALU.is_equal))
                    yield
                    if k == 0:
                        V.tensor_scalar(tok_run[:, :], tok_run[:, :], float(BLK), None, ALU.add)
                        V.tensor_scalar(pay[q][:, :, D + 1], r1[:, :], -1.0, float(NE), ALU.mult, ALU.add)
                        V.tensor_tensor(rx[:, :, 0:NE], lg[:, :, :], bc(l_max[:, :]), ALU.subtract)
                        ch.did(V.scalar_tensor_tensor(lg2[:, :, :], hot[:, 0, :, :], -BIG, lg[:, :, :], ALU.mult, ALU.add))
                        yield
                V.tensor_tensor(rx[:, :, NE], l_max2[:, :], l_max[:, :], ALU.subtract)
                V.tensor_tensor(hot_any[:, :, :], hot[:, 0, :, :], hot[:, 1, :, :], ALU.add).then_inc(s.hot_ready, 1)

            def low_parts(L, n, q):
                ff, pay16 = (xff if L == 0 else xt), pay[q][:, :, :].bitcast(F16)
                dve.wait_ge(SL[L].hi_ready, n + 1)
                return V.scalar_tensor_tensor(pay16[:, :, D:2 * D], ff[:, :, :], S_X, pay16[:, :, 0:D], ALU.mult, ALU.subtract)

            def places(L, n, q):
                s = SL[L]
                dve.wait_ge(s.rank_done, n + 1)
                dve.wait_ge(s.rexp, n + 1)
                ch.did(V.tensor_tensor(pos[:, :, :], rank_ps.rearrange("p (t e) -> p t e", e=NE),
                                       base_run[L][:, :].unsqueeze(1).to_broadcast([P, TILES, NE]), ALU.add))
                if L == 0:
                    ch.did(V.tensor_scalar(den[:, :], rex[:, :, NE], 1.0, None, ALU.add))
                else:
                    ch.did(V.tensor_reduce(den[:, :], rex[:, :, 0:NE], AX_X, ALU.add))
                yield
                V.tensor_tensor(base_run[L][:, :], base_run[L][:, :], tot_ps, ALU.add)
                for k in range(TOP):
                    V.tensor_tensor(hot_pos[:, k, :, :], hot[:, k, :, :], pos[:, :, :], ALU.mult)
                ch.did(V.reciprocal(x1w[q][:, :, D], den[:, :]))
                yield
                V.tensor_tensor(x1w[q][:, :, D + 1], x1w[q][:, :, D], rex[:, :, NE], ALU.mult).then_inc(s.x1w_ready, 1)
                ch.did(V.tensor_reduce(slot_f[:, :, :], hot_pos[:, :, :, :], AX_X, ALU.add))
                yield
                copied = V.tensor_copy(slot[q][:, :, :], slot_f[:, :, :])
                if L == 1:
                    copied.then_inc(s.slots_ready, 1)
                else:
                    ch.did(copied)

            def blocks(L):
                s = SL[L]

                def statistics_of(n, q, has_input, has_ff, beside):
                    srcs = [xin[q][:, :, 0:D]] if has_input else []
                    if has_ff:
                        dve.wait_ge(s.xt_ready, 2 * n - 2)
                        srcs.append(xt)
                    at = 0 if has_input else TILES
                    if srcs:
                        statistics(srcs, rstd1[:, at:], nmr1[:, at:], beside).then_inc(s.st1, 1)
                    finish_steps(beside)

                def step(i, d):
                    n, q, turn = block_at(i, d)
                    first, before_last, last, over = (
                        [n == m for m in (0, NBLK - 2, NBLK - 1, NBLK)] if isinstance(n, int) else [False] * 4)
                    if not (last or over):
                        take_in(L, *block_at(i, d + 1))
                    statistics_of(n + 1, (q + 1) % 2, not (last or over), L == 0 and not first,
                                  iter(()) if first else route(L, *block_at(i, d - 1)))
                    if not first and L == 1:
                        ch.did(low_parts(L, n - 1, (q + 1) % 2))
                    placing = iter(()) if first else places(L, n - 1, (q + 1) % 2)
                    if not over:
                        add_attention(L, n, q, turn, placing)
                    finish_steps(placing)
                    if not first and L == 0:
                        low_parts(L, n - 1, (q + 1) % 2).then_inc(s.slots_ready, 1)
                    if not (before_last or last or over):
                        arrive(L, *block_at(i, d + 2))
                    if not (last or over):
                        scores(L, n + 1)
                arrive(L, 0, 0, 0)
                take_in(L, 0, 0, 0)
                statistics_of(0, 0, True, False, iter(()))
                split_second(L)
                arrive(L, 1, 1, 0)
                scores(L, 0)
                step(0, 0)
                dve.wait_ge(rt_in, 16 * 6)
                with dve.Fori(0, NBLK // per - 2) as i:
                    ch.loop(i, 0, DVE_SIGNALS[L])
                    for d in (1, 2):
                        step(i, d)
                ch.looped(NBLK // per - 2, DVE_SIGNALS[L])
                for n in range(NBLK - 3, NBLK + 1):
                    step(0, n)

            def group_tables(L):
                s = SL[L]
                dve.wait_ge(s.slots_ready, NBLK)
                base0 = cst[:, C_BASE:C_BASE + NE]
                V.tensor_copy(end_i[:, :], base_run[L][:, :])
                ch.did(V.tensor_tensor(cnt[:, :], base_run[L][:, :], base0, ALU.subtract))
                ch.wait()
                ch.did(V.tensor_scalar(cnt_i[:, :], cnt[:, :], float(GRP - 1), None, ALU.add))
                ch.wait()
                ch.did(V.tensor_scalar(cnt_i[:, :], cnt_i[:, :], 8, None, ALU.logical_shift_right))
                ch.wait()
                ch.did(V.tensor_copy(ng_e[:, :], cnt_i[:, :]))
                ch.wait()
                ch.did(V.tensor_tensor_scan(cum[:, :], one8[:, :], ng_e[:, :], 0.0, ALU.mult, ALU.add))
                ch.wait()
                g_no = cst[:, C_G:C_G + NG]
                wide = [P, NG, NE]
                ch.did(V.tensor_tensor(past[:, :, :], cum[:, :].unsqueeze(1).to_broadcast(wide),
                                       g_no.unsqueeze(2).to_broadcast(wide), ALU.is_le))
                ch.wait()
                V.tensor_reduce(grp_e[:, :], past[:, :, :], AX_X, ALU.add)
                ch.did(V.tensor_tensor(past_n[:, :, :], past[:, :, :], ng_e[:, :].unsqueeze(1).to_broadcast(wide), ALU.mult))
                ch.wait()
                ch.did(V.tensor_reduce(grp_b[:, :], past_n[:, :, :], AX_X, ALU.add))
                ch.wait()
                V.tensor_scalar(grp_r[:, :], grp_e[:, :], float(CAP), None, ALU.mult)
                ch.did(V.tensor_tensor(grp_c[:, :], g_no, grp_b[:, :], ALU.subtract))
                ch.wait()
                V.tensor_scalar(grp_ei[:, :], grp_e[:, :], float(NE - 1), None, ALU.min)
                ch.did(V.scalar_tensor_tensor(grp_b[:, :], grp_c[:, :], float(GRP), grp_r[:, :], ALU.mult, ALU.add))
                ch.wait()
                V.tensor_copy(grp_ri[:, :], grp_b[:, :]).then_inc(s.tables, 1)

            def split_second(L):
                dve.wait_ge(stage_in, 16 * (2 * L + 1))
                st = w_stage[:, 0:NE * NC[L] * D].rearrange("p (ec d) -> p ec d", d=D)
                hi, lo = (w2[L][:, :, :, k, :].rearrange("p e c d -> p (e c) d") for k in range(2))
                ch.did(V.tensor_scalar(hi, st, S_W, None, ALU.mult))
                ch.wait()
                V.scalar_tensor_tensor(lo, st, S_W, hi, ALU.mult, ALU.subtract).then_inc(stage_used, 1)

            def split_first(L):
                dve.wait_ge(stage_in, 16 * (2 * L + 2))
                if L == 0:
                    dve.wait_ge(bw_ps, 1)
                    V.tensor_tensor(b1_cols[0][:, :], bank[0][:, 0:NE * NC[0]], vec_cols[:, 0:NE * NC[0]], ALU.add)
                for part in range(2):
                    for e in range(NE):
                        st = w_stage[:, e * HID[L]:(e + 1) * HID[L]]
                        scale = gain[:, e:e + 1] if L == 0 else S_W
                        if part == 0:
                            last = V.tensor_scalar(w1[L][:, e, 0, :], st, scale, None, ALU.mult)
                        else:
                            last = V.scalar_tensor_tensor(w1[L][:, e, 1, :], st, scale, w1[L][:, e, 0, :], ALU.mult, ALU.subtract)
                    if part == 0:
                        ch.did(last)
                        ch.wait()
                last.then_inc(w_ready[L], 1)
                dve.wait_ge(w_ready[L], 1)
                V.memset(g_k[:, :], 0.0).then_inc(stage_used, 1)
                dve.wait_ge(stage_used, 2 * (L + 1))

            def groups(L):
                s = SL[L]
                half = NC[L] // 2

                def place(g, k, turn):
                    dve.wait_ge(s.g_loaded[k], 16 * (turn + 1))
                    wait_past(dve, s.placed, g)
                    ch.did(V.tensor_scalar(g_k[:, :], g_in[k][:, :, D + 1], grp_e[:, bass.ds(g, 1)], float(N_TOK),
                                           ALU.not_equal, ALU.mult))
                    ch.wait()
                    V.tensor_tensor(g_row[k][:, :], g_k[:, :], g_in[k][:, :, D], ALU.add).then_inc(s.placed, 1)

                def split(g, k):
                    part = [slice(2 * hf, 2 * hf + 2) for hf in range(half)]
                    a = g_act[k % 2]
                    for hf in range(half):
                        dve.wait_ge(s.act_done, NC[L] * g + 2 * hf + 2)
                        ch.did(V.tensor_scalar(g_h[k][:, 0, part[hf], :], a[:, part[hf], :], S_H, None, ALU.mult))
                    for hf in range(half):
                        if hf == 0:
                            ch.wait()
                        V.scalar_tensor_tensor(g_h[k][:, 1, part[hf], :], a[:, part[hf], :], S_H,
                                               g_h[k][:, 0, part[hf], :], ALU.mult, ALU.subtract).then_inc(s.h_split, 1)

                def experts(g, n):
                    return table_values(mybir.EngineType.DVE, grp_ei, g, n, NE - 1)

                def finish(g, k, turn, e):
                    wait_past(dve, s.y_out[k], 16 * GT * turn)
                    dve.wait_ge(s.placed, g + 1)
                    V.tensor_copy(g_dst[k][:, :], g_row[k][:, :])
                    dve.wait_ge(s.y_done, g + 1)
                    flat = b2_bc[L][:, :, :].rearrange("p e d -> p (e d)")
                    V.scalar_tensor_tensor(g_y[k][:, :, :], bank[5 + k % 2][:, 0:GT * D].rearrange("p (t d) -> p t d", d=D),
                                           1.0 / (S_H * S_W), flat[:, bass.ds(e * D, D)].unsqueeze(1).to_broadcast([P, GT, D]),
                                           ALU.mult, ALU.add).then_inc(s.y_ready, 1)
                for k in range(2):
                    place(k, k, 0)
                    split(k, k)
                turn_signals = SPAN * (half + 1)
                per_turn = SPAN // AHEAD

                def turn(i, last=False):
                    n = TAIL if last else SPAN
                    es = experts(SPAN * i, n)
                    for k in range(n):
                        g, a = SPAN * i + k, (k + 2) % AHEAD
                        if not last or k + 2 < n:
                            place(g + 2, a, per_turn * i + (k + 2) // AHEAD)
                            split(g + 2, a)
                        finish(g, k % AHEAD, per_turn * i + k // AHEAD, es[k])
                turn(0)
                with dve.Fori(1, TURNS) as i:
                    ch.loop(i, 1, turn_signals)
                    turn(i)
                ch.looped(TURNS - 1, turn_signals)
                turn(TURNS, last=True)

            for L in range(2):
                blocks(L)
                if L == 0:
                    ch.did(V.tensor_copy(tok_run[:, :], cst[:, C_TOK:C_TOK + TILES]))
                group_tables(L)
                split_first(L)
                groups(L)
            for n in range(NBLK):
                dve.wait_ge(fin_in[n], 48)
                add_experts(fin_x[n], fin_y[n % len(fin_y)]).then_inc(fin_done, 1)



_INS = ['x', 'adj', 'L0_gnn_W', 'L0_gnn_a_src', 'L0_gnn_a_dst', 'L0_ffn_Wr', 'L0_ffn_br', 'L0_ffn_ln_g', 'L0_ffn_ln_b',
        'L0_ffn_W1', 'L0_ffn_b1', 'L0_ffn_W2', 'L0_ffn_b2', 'L1_gnn_W', 'L1_gnn_a', 'L1_ffn_gate_w', 'L1_ffn_gate_b',
        'L1_ffn_W1', 'L1_ffn_b1', 'L1_ffn_W2', 'L1_ffn_b2']


def kernel(**inputs):
    import numpy as _np
    import concourse.bacc as _bacc
    from concourse import mybir as _mybir
    from concourse.bass_utils import run_bass_kernel_spmd as _run

    nc = _bacc.Bacc("TRN2", target_bir_lowering=False, num_devices=1)
    arrays, args = {}, []
    for name in _INS:
        a = _np.ascontiguousarray(inputs[name])
        if name in ('x', 'adj'):
            a = a.reshape(N_TOK, a.shape[-1])
        arrays[f"in_{name}_dram"] = a
        args.append(nc.dram_tensor(f"in_{name}_dram", a.shape, _mybir.dt.from_np(a.dtype), kind="ExternalInput").ap())
    c = _np.zeros((P, C_END), _np.float32)
    c[:, C_ID:C_ID + P] = _np.eye(P)
    c[:, C_TRI:C_TRI + P] = _np.triu(_np.ones((P, P)), 1)
    c[:, C_REV:C_REV + TILES * NE] = _np.tile(NE - _np.arange(NE), TILES)
    c[:, C_TOK:C_TOK + TILES] = _np.arange(TILES) * P + _np.arange(P)[:, None]
    c[:, C_BASE:C_BASE + NE] = _np.arange(NE) * CAP
    c[:, C_G:C_G + NG] = _np.arange(NG)
    arrays["in_consts_dram"] = c
    args.append(nc.dram_tensor("in_consts_dram", c.shape, F32, kind="ExternalInput").ap())
    args.append(nc.dram_tensor("out_0_dram", (N_TOK, D), F32, kind="ExternalOutput").ap())
    gnn_moe_kernel(nc, *args)
    r = _run(nc, [arrays], core_ids=[0])
    return r.results[0]["out_0_dram"].reshape(128, NODES, D)
```
